# Optimizing a Trainium2 kernel written in Bass

```python
import numpy as np
import jax
import jax.numpy as jnp

def _softmax(x, axis=-1):
    return jax.nn.softmax(x, axis=axis)

def _gelu(x):
    return jax.nn.gelu(x, approximate=True)

def _silu(x):
    return jax.nn.silu(x)

def _sigmoid(x):
    return jax.nn.sigmoid(x)

def _layernorm(x, axis=-1, eps=1e-05):
    m = jnp.mean(x, axis=axis, keepdims=True)
    v = jnp.var(x, axis=axis, keepdims=True)
    return (x - m) / jnp.sqrt(v + eps)

def _scatter_add(tgt, idx, src, axis=0):
    return tgt.at[idx].add(src)

def _segment_sum(src, seg, n):
    return jax.ops.segment_sum(src, seg, n)
kernel_name = 'mk_gnn_resnorm_d4_gnn_r8_c846ea'

def setup_inputs(seed: int=0):
    np.random.seed(seed)
    _w = jnp.asarray

    def _rec_inputs():
        import jax
        import jax.numpy as jnp
        _gk = jax.random.key(seed)
        x = -0.0005121 + 1.001 * jax.random.normal(jax.random.fold_in(_gk, 1), (12500, 64), jnp.float32)
        _s = jax.random.randint(jax.random.fold_in(_gk, 2), (100000,), 0, 12500, jnp.int32)
        _d = jax.random.randint(jax.random.fold_in(_gk, 3), (100000,), 0, 12500, jnp.int32)
        _loop = jnp.arange(12500, dtype=jnp.int32)
        src = jnp.concatenate([_s, _d, _loop])
        dst = jnp.concatenate([_d, _s, _loop])
        _o = jnp.argsort(dst, stable=True)
        src = src[_o]
        dst = dst[_o]
        edge_type_4 = jax.random.randint(jax.random.fold_in(_gk, 13), (212500,), 0, 4, jnp.int32)
        edge_weight = jax.random.uniform(jax.random.fold_in(_gk, 14), (212500,), jnp.float32, 0.0, 1)
        return (x, src, dst, edge_type_4, edge_weight)
    x, src, dst, edge_type_4, edge_weight = _rec_inputs()

    def _L0_gnn_setup():
        import jax, jax.numpy as jnp
        import numpy as np
        N = 6250
        E = 100000
        H = 64
        K = 4
        STEPS = 4

        def _gru_cell(a, feat, w_ih, w_hh, b_ih, b_hh):
            gi = a @ w_ih.T + b_ih
            gh = feat @ w_hh.T + b_hh
            i_r, i_z, i_n = jnp.split(gi, 3, axis=-1)
            h_r, h_z, h_n = jnp.split(gh, 3, axis=-1)
            r = jax.nn.sigmoid(i_r + h_r)
            z = jax.nn.sigmoid(i_z + h_z)
            n = jnp.tanh(i_n + r * h_n)
            return (1.0 - z) * n + z * feat
        key = jax.random.key(seed)
        ks = jax.random.split(key, 10)
        s = 0.05
        return {'h': jax.random.normal(ks[0], (N, H), jnp.float32), 'W': jax.random.normal(ks[1], (K, H, H), jnp.float32) * s, 'b': jax.random.normal(ks[2], (K, H), jnp.float32) * s, 'w_ih': jax.random.normal(ks[3], (3 * H, H), jnp.float32) * s, 'w_hh': jax.random.normal(ks[4], (3 * H, H), jnp.float32) * s, 'b_ih': jax.random.normal(ks[5], (3 * H,), jnp.float32) * s, 'b_hh': jax.random.normal(ks[6], (3 * H,), jnp.float32) * s, 'src': jax.random.randint(ks[7], (E,), 0, N, dtype=jnp.int32), 'dst': jax.random.randint(ks[8], (E,), 0, N, dtype=jnp.int32), 'etypes': jax.random.randint(ks[9], (E,), 0, K, dtype=jnp.int32)}
    _L0_gnn_all = _L0_gnn_setup()
    _L0_gnn_in = {k: v for k, v in _L0_gnn_all.items() if k in ('W', 'b', 'w_ih', 'w_hh', 'b_ih', 'b_hh')}
    del _L0_gnn_all

    def _L1_gnn_setup():
        import jax, jax.numpy as jnp
        import numpy as np
        N_NODES = 6250
        N_EDGES = 100000
        D_IN, D_HID, D_OUT = (64, 128, 64)

        def _glorot(key, fan_in, fan_out):
            lim = (6.0 / (fan_in + fan_out)) ** 0.5
            return jax.random.uniform(key, (fan_in, fan_out), jnp.float32, -lim, lim)

        def _gin_conv(x, src, dst, Wa, ba, Wb, bb):
            msgs = x[src]
            agg = jax.ops.segment_sum(msgs, dst, num_segments=x.shape[0])
            h = x + agg
            h = jax.nn.relu(h @ Wa + ba)
            return h @ Wb + bb
        key = jax.random.key(seed)
        ks = jax.random.split(key, 10)
        x = jax.random.normal(ks[0], (N_NODES, D_IN), jnp.float32)
        edge_index = jax.random.randint(ks[1], (2, N_EDGES), 0, N_NODES, jnp.int64)
        W1a = _glorot(ks[2], D_IN, D_HID)
        b1a = jnp.zeros((D_HID,), jnp.float32)
        W1b = _glorot(ks[3], D_HID, D_HID)
        b1b = jnp.zeros((D_HID,), jnp.float32)
        W2a = _glorot(ks[4], D_HID, D_HID)
        b2a = jnp.zeros((D_HID,), jnp.float32)
        W2b = _glorot(ks[5], D_HID, D_OUT)
        b2b = jnp.zeros((D_OUT,), jnp.float32)
        return {'x': x, 'edge_index': edge_index, 'W1a': W1a, 'b1a': b1a, 'W1b': W1b, 'b1b': b1b, 'W2a': W2a, 'b2a': b2a, 'W2b': W2b, 'b2b': b2b}
    _L1_gnn_all = _L1_gnn_setup()
    _L1_gnn_in = {k: v for k, v in _L1_gnn_all.items() if k in ('W1a', 'b1a', 'W1b', 'b1b', 'W2a', 'b2a', 'W2b', 'b2b')}
    del _L1_gnn_all

    def _L2_gnn_setup():
        import jax, jax.numpy as jnp
        import numpy as np
        N_NODES = 12500
        D_IN = 64
        D_OUT = 64
        N_EDGES = 400000
        BN_EPS = 1e-05

        def _gcn_conv(x, W, b, edge_index, n_nodes):
            loops = jnp.arange(n_nodes, dtype=edge_index.dtype)
            src = jnp.concatenate([edge_index[0], loops])
            dst = jnp.concatenate([edge_index[1], loops])
            deg = jax.ops.segment_sum(jnp.ones_like(dst, dtype=x.dtype), dst, num_segments=n_nodes)
            deg_inv_sqrt = jnp.where(deg > 0, jax.lax.rsqrt(jnp.maximum(deg, 1.0)), 0.0)
            norm = deg_inv_sqrt[src] * deg_inv_sqrt[dst]
            h = x @ W
            msg = h[src] * norm[:, None]
            out = jax.ops.segment_sum(msg, dst, num_segments=n_nodes)
            return out + b

        def _batchnorm1d(x, gamma, beta):
            mean = jnp.mean(x, axis=0)
            var = jnp.mean(jnp.square(x - mean), axis=0)
            return (x - mean) * jax.lax.rsqrt(var + BN_EPS) * gamma + beta
        key = jax.random.key(seed)
        k1, k2, k3, k4 = jax.random.split(key, 4)
        x = jax.random.normal(k1, (N_NODES, D_IN), dtype=jnp.float32)
        edge_index = jax.random.randint(k2, (2, N_EDGES), 0, N_NODES, dtype=jnp.int64)
        W = jax.random.normal(k3, (D_IN, D_OUT), dtype=jnp.float32) / np.sqrt(D_IN)
        b = jnp.zeros((D_OUT,), dtype=jnp.float32)
        gamma = jnp.ones((D_OUT,), dtype=jnp.float32)
        beta = jnp.zeros((D_OUT,), dtype=jnp.float32)
        return {'x': x, 'W': W, 'b': b, 'gamma': gamma, 'beta': beta, 'edge_index': edge_index}
    _L2_gnn_all = _L2_gnn_setup()
    _L2_gnn_in = {k: v for k, v in _L2_gnn_all.items() if k in ('W', 'b', 'gamma', 'beta')}
    del _L2_gnn_all

    def _L3_gnn_setup():
        import jax, jax.numpy as jnp
        import numpy as np
        N_NODES = 6250
        N_EDGES = 100000
        D_IN = 64
        D_OUT = 64
        key = jax.random.key(seed)
        ks = jax.random.split(key, 8)
        feat = jax.random.normal(ks[0], (N_NODES, D_IN), dtype=jnp.float32)
        weight = jax.random.uniform(ks[1], (N_EDGES,), dtype=jnp.float32)
        W_self = jax.random.normal(ks[2], (D_OUT, D_IN), dtype=jnp.float32) * 0.1
        b_self = jax.random.normal(ks[3], (D_OUT,), dtype=jnp.float32) * 0.1
        W_neigh = jax.random.normal(ks[4], (D_OUT, D_IN), dtype=jnp.float32) * 0.1
        b_neigh = jax.random.normal(ks[5], (D_OUT,), dtype=jnp.float32) * 0.1
        src = jax.random.randint(ks[6], (N_EDGES,), 0, N_NODES, dtype=jnp.int64)
        dst = jax.random.randint(ks[7], (N_EDGES,), 0, N_NODES, dtype=jnp.int64)
        return {'feat': feat, 'weight': weight, 'W_self': W_self, 'b_self': b_self, 'W_neigh': W_neigh, 'b_neigh': b_neigh, 'src': src, 'dst': dst}
    _L3_gnn_all = _L3_gnn_setup()
    _L3_gnn_in = {k: v for k, v in _L3_gnn_all.items() if k in ('W_self', 'b_self', 'W_neigh', 'b_neigh')}
    del _L3_gnn_all
    return {'x': x, 'src': src, 'dst': dst, 'edge_type_4': edge_type_4, 'edge_weight': edge_weight, 'L0_gnn_W': _L0_gnn_in['W'], 'L0_gnn_b': _L0_gnn_in['b'], 'L0_gnn_w_ih': _L0_gnn_in['w_ih'], 'L0_gnn_w_hh': _L0_gnn_in['w_hh'], 'L0_gnn_b_ih': _L0_gnn_in['b_ih'], 'L0_gnn_b_hh': _L0_gnn_in['b_hh'], 'L1_gnn_W1a': _L1_gnn_in['W1a'], 'L1_gnn_b1a': _L1_gnn_in['b1a'], 'L1_gnn_W1b': _L1_gnn_in['W1b'], 'L1_gnn_b1b': _L1_gnn_in['b1b'], 'L1_gnn_W2a': _L1_gnn_in['W2a'], 'L1_gnn_b2a': _L1_gnn_in['b2a'], 'L1_gnn_W2b': _L1_gnn_in['W2b'], 'L1_gnn_b2b': _L1_gnn_in['b2b'], 'L2_gnn_W': _L2_gnn_in['W'], 'L2_gnn_b': _L2_gnn_in['b'], 'L2_gnn_gamma': _L2_gnn_in['gamma'], 'L2_gnn_beta': _L2_gnn_in['beta'], 'L3_gnn_W_self': _L3_gnn_in['W_self'], 'L3_gnn_b_self': _L3_gnn_in['b_self'], 'L3_gnn_W_neigh': _L3_gnn_in['W_neigh'], 'L3_gnn_b_neigh': _L3_gnn_in['b_neigh']}

def reference(x, src, dst, edge_type_4, edge_weight, L0_gnn_W, L0_gnn_b, L0_gnn_w_ih, L0_gnn_w_hh, L0_gnn_b_ih, L0_gnn_b_hh, L1_gnn_W1a, L1_gnn_b1a, L1_gnn_W1b, L1_gnn_b1b, L1_gnn_W2a, L1_gnn_b2a, L1_gnn_W2b, L1_gnn_b2b, L2_gnn_W, L2_gnn_b, L2_gnn_gamma, L2_gnn_beta, L3_gnn_W_self, L3_gnn_b_self, L3_gnn_W_neigh, L3_gnn_b_neigh):
    import jax
    import jax.numpy as jnp

    def _L0_gnn_ref(h, W, b, w_ih, w_hh, b_ih, b_hh, src, dst, etypes):
        import jax, jax.numpy as jnp
        import numpy as np
        N = 6250
        E = 100000
        H = 64
        K = 4
        STEPS = 4

        def _gru_cell(a, feat, w_ih, w_hh, b_ih, b_hh):
            gi = a @ w_ih.T + b_ih
            gh = feat @ w_hh.T + b_hh
            i_r, i_z, i_n = jnp.split(gi, 3, axis=-1)
            h_r, h_z, h_n = jnp.split(gh, 3, axis=-1)
            r = jax.nn.sigmoid(i_r + h_r)
            z = jax.nn.sigmoid(i_z + h_z)
            n = jnp.tanh(i_n + r * h_n)
            return (1.0 - z) * n + z * feat
        num_nodes = h.shape[0]

        def step(feat, _):
            transformed = jnp.einsum('nd,khd->knh', feat, W) + b[:, None, :]
            msgs = transformed[etypes, src]
            a = jax.ops.segment_sum(msgs, dst, num_segments=num_nodes)
            feat = _gru_cell(a, feat, w_ih, w_hh, b_ih, b_hh)
            return (feat, None)
        feat, _ = jax.lax.scan(step, h, None, length=STEPS)
        return feat

    def _L1_gnn_ref(x, edge_index, W1a, b1a, W1b, b1b, W2a, b2a, W2b, b2b):
        import jax, jax.numpy as jnp
        import numpy as np
        N_NODES = 6250
        N_EDGES = 100000
        D_IN, D_HID, D_OUT = (64, 128, 64)

        def _glorot(key, fan_in, fan_out):
            lim = (6.0 / (fan_in + fan_out)) ** 0.5
            return jax.random.uniform(key, (fan_in, fan_out), jnp.float32, -lim, lim)

        def _gin_conv(x, src, dst, Wa, ba, Wb, bb):
            msgs = x[src]
            agg = jax.ops.segment_sum(msgs, dst, num_segments=x.shape[0])
            h = x + agg
            h = jax.nn.relu(h @ Wa + ba)
            return h @ Wb + bb
        src, dst = (edge_index[0], edge_index[1])
        h = jax.nn.relu(_gin_conv(x, src, dst, W1a, b1a, W1b, b1b))
        h = jax.nn.relu(_gin_conv(h, src, dst, W2a, b2a, W2b, b2b))
        return h

    def _L2_gnn_ref(x, W, b, gamma, beta, edge_index):
        import jax, jax.numpy as jnp
        import numpy as np
        N_NODES = 12500
        D_IN = 64
        D_OUT = 64
        N_EDGES = 400000
        BN_EPS = 1e-05

        def _gcn_conv(x, W, b, edge_index, n_nodes):
            loops = jnp.arange(n_nodes, dtype=edge_index.dtype)
            src = jnp.concatenate([edge_index[0], loops])
            dst = jnp.concatenate([edge_index[1], loops])
            deg = jax.ops.segment_sum(jnp.ones_like(dst, dtype=x.dtype), dst, num_segments=n_nodes)
            deg_inv_sqrt = jnp.where(deg > 0, jax.lax.rsqrt(jnp.maximum(deg, 1.0)), 0.0)
            norm = deg_inv_sqrt[src] * deg_inv_sqrt[dst]
            h = x @ W
            msg = h[src] * norm[:, None]
            out = jax.ops.segment_sum(msg, dst, num_segments=n_nodes)
            return out + b

        def _batchnorm1d(x, gamma, beta):
            mean = jnp.mean(x, axis=0)
            var = jnp.mean(jnp.square(x - mean), axis=0)
            return (x - mean) * jax.lax.rsqrt(var + BN_EPS) * gamma + beta
        h = _gcn_conv(x, W, b, edge_index, x.shape[0])
        h = jax.nn.relu(h)
        return _batchnorm1d(h, gamma, beta)

    def _L3_gnn_ref(feat, weight, W_self, b_self, W_neigh, b_neigh, src, dst):
        import jax, jax.numpy as jnp
        import numpy as np
        N_NODES = 6250
        N_EDGES = 100000
        D_IN = 64
        D_OUT = 64
        n = feat.shape[0]
        msg = feat[src] * weight[:, None]
        neigh_sum = jax.ops.segment_sum(msg, dst, num_segments=n)
        deg = jax.ops.segment_sum(jnp.ones_like(weight), dst, num_segments=n)
        h_neigh = neigh_sum / jnp.maximum(deg, 1.0)[:, None]
        rst = feat @ W_self.T + b_self + (h_neigh @ W_neigh.T + b_neigh)
        return rst
    edge_index = jnp.stack([src, dst])
    x = _layernorm(x + _L0_gnn_ref(x, L0_gnn_W, L0_gnn_b, L0_gnn_w_ih, L0_gnn_w_hh, L0_gnn_b_ih, L0_gnn_b_hh, src, dst, edge_type_4), axis=-1)
    x = _layernorm(x + _L1_gnn_ref(x, edge_index, L1_gnn_W1a, L1_gnn_b1a, L1_gnn_W1b, L1_gnn_b1b, L1_gnn_W2a, L1_gnn_b2a, L1_gnn_W2b, L1_gnn_b2b), axis=-1)
    x = _layernorm(x + _L2_gnn_ref(x, L2_gnn_W, L2_gnn_b, L2_gnn_gamma, L2_gnn_beta, edge_index), axis=-1)
    x = _layernorm(x + _L3_gnn_ref(x, edge_weight, L3_gnn_W_self, L3_gnn_b_self, L3_gnn_W_neigh, L3_gnn_b_neigh, src, dst), axis=-1)
    return x

_drawn_inputs = setup_inputs


def setup_inputs(seed=0):
    import zlib

    import numpy as np

    out = dict(_drawn_inputs(seed))
    spreads = {'L1_gnn_b1a': (0.0, 0.1),
     'L1_gnn_b1b': (0.0, 0.1),
     'L1_gnn_b2a': (0.0, 0.528),
     'L1_gnn_b2b': (0.0, 0.526),
     'L2_gnn_b': (0.0, 0.1),
     'L2_gnn_gamma': (1.0, 0.2),
     'L2_gnn_beta': (0.0, 0.1)}
    factors = {}
    for name, (base, spread) in spreads.items():
        noise = np.random.default_rng([zlib.crc32(name.encode()), seed]).standard_normal(out[name].shape)
        drawn = base * np.exp(spread * noise) if base else spread * noise
        out[name] = jnp.asarray(drawn.astype(out[name].dtype))
    for name, factor in factors.items():
        out[name] = (out[name] * factor).astype(out[name].dtype)
    return out
```

```python
import concourse.bass as bass
from concourse import mybir
from contextlib import ExitStack

N = 12500
H = 64
E = 212500
K = 4
HID = 128
P = 128
NT = -(-N // P)
NP = NT * P
LAST = N - (NT - 1) * P
RING = 64
GROUP = 8
BLOCK = 32
TP = -(-E // (P * RING)) * RING
FULL = E // P
TR = TP // P
ROUNDS = TP // RING
OHS = 16
STEPS = 4
GIN1, GIN2, GCN, SAGE = 4, 5, 6, 7
PASSES = 8
EPS = 1e-5
CH = 14
NCH = NT // CH
NO_NODE = 20000


def build(nc, x, src, dst, edge_type, edge_weight, g_W, g_b, g_w_ih, g_w_hh, g_b_ih, g_b_hh,
          W1a, b1a, W1b, b1b, W2a, b2a, W2b, b2b, gcn_W, gcn_b, gamma, beta,
          W_self, b_self, W_neigh, b_neigh, out):
    fp32, bf16, i32 = mybir.dt.float32, mybir.dt.bfloat16, mybir.dt.int32
    ALU, ACT, AX = mybir.AluOpType, mybir.ActivationFunctionType, mybir.AxisListType
    ds = bass.ds

    typed = [nc.dram_tensor(f"typed_table{i}", [NP * K, 3 * H], bf16) for i in range(2)]
    gin1_table = nc.dram_tensor("gin1_table", [NP, 3 * H], bf16)
    gin2_table = nc.dram_tensor("gin2_table", [NP, 3 * HID], bf16)
    gcn_table = nc.dram_tensor("gcn_table", [NP, 3 * H], bf16)
    sage_table = nc.dram_tensor("sage_table", [NP, 3 * H], bf16)
    tables = [typed[0], typed[1], typed[0], typed[1], gin1_table, gin2_table, gcn_table, sage_table]

    def width(p):
        return HID if p == GIN2 else H

    ctx = ExitStack()
    with ctx:
        def sb(name, shape, dt):
            return ctx.enter_context(nc.sbuf_tensor(name, shape, dt))

        def bank(name):
            return ctx.enter_context(nc.psum_tensor(name, [P, 512], fp32))

        def sem(name):
            return ctx.enter_context(nc.semaphore(name))

        x_all = sb("x_all", [P, NT, H], fp32)
        h_all = sb("h_all", [P, NT, H], fp32)
        big = sb("big", [P, NT * P], fp32)
        ring = sb("ring", [P, RING * 3 * H], bf16)
        onehot = sb("onehot", [P, OHS, 3 * P], bf16)
        onehot_edge = sb("onehot_edge", [P, 3 * P], bf16)
        typed_idx = sb("typed_idx", [P, TP], i32)
        src_idx = sb("src_idx", [P, TP], i32)
        dst_f = sb("dst_f", [P, TP], fp32)
        w_f = sb("w_f", [P, TP], fp32)
        idx_stage = sb("idx_stage", [P, 2, BLOCK], i32)
        zeros = sb("zeros", [P, 3 * HID], bf16)
        ones_bf = sb("ones_bf", [P, 1], bf16)
        ones_row = sb("ones_row", [1, P], fp32)
        ones_mean = sb("ones_mean", [P, P], fp32)
        eps_col = sb("eps_col", [P, 1], fp32)
        iota_row = sb("iota_row", [P, P], fp32)
        iota_col = sb("iota_col", [P, 1], fp32)
        bound_col = sb("bound_col", [P, 1], fp32)
        ident = sb("ident", [P, P], fp32)
        pick_last = sb("pick_last", [P, NT], fp32)
        mask_last = sb("mask_last", [P, 1], fp32)
        node_ids = sb("node_ids", [P, P], fp32)
        open_col = sb("open_col", [P, 1], fp32)
        first_open = sb("first_open", [1, NT + 1], i32)
        count = sb("count", [P, NT], fp32)
        inv_count = sb("inv_count", [P, NT], fp32)
        deg_rsqrt = sb("deg_rsqrt", [P, NT], fp32)
        agg_sum = sb("agg_sum", [P, HID], fp32)
        aggT = sb("aggT", [H + 1, P], fp32)
        aggT_wide = sb("aggT_wide", [P, P], fp32)
        hT_cur = sb("hT_cur", [H + 1, P], fp32)
        hT_new = sb("hT_new", [H + 1, P], fp32)
        gates = sb("gates", [P, 2 * H], fp32)
        cand = sb("cand", [P, H], fp32)
        cand_act = sb("cand_act", [P, H], fp32)
        diff = sb("diff", [P, H], fp32)
        row_new = sb("row_new", [P, HID], fp32)
        y_row = sb("y_row", [P, H], fp32)
        v_row = sb("v_row", [P, H], fp32)
        o_row = sb("o_row", [P, H], fp32)
        out_row = sb("out_row", [P, H], fp32)
        uT = sb("uT", [P, P], fp32)
        rest = sb("rest", [P, K * H], fp32)
        stage = sb("stage", [P, K, 3 * H], bf16)
        stats6 = sb("stats6", [P, nc.vector.BN_STATS_DIM], fp32)
        moments = sb("moments", [P, 2], fp32)
        std = sb("std", [P, NT], fp32)
        rstd = sb("rstd", [P, 1], fp32)
        typed_w = sb("typed_w", [H + 1, K * H], fp32)
        gate_in_w = sb("gate_in_w", [H + 1, 4 * H], fp32)
        gate_h_w = sb("gate_h_w", [H + 1, 4 * H], fp32)
        raw_w = sb("raw_w", [P, 8, H], fp32)
        w1a = sb("w1a", [H, HID], fp32)
        w1b = sb("w1b", [HID, HID], fp32)
        w2a = sb("w2a", [HID, HID], fp32)
        w2b = sb("w2b", [HID, H], fp32)
        b1a_col = sb("b1a_col", [HID, 1], fp32)
        b2a_col = sb("b2a_col", [HID, 1], fp32)
        rows = sb("rows", [1, HID + 3 * H], fp32)
        b1b_row, b2b_row = rows[0:1, 0:HID], rows[0:1, HID:HID + H]
        b_self_row, b_neigh_row = rows[0:1, HID + H:HID + 2 * H], rows[0:1, HID + 2 * H:HID + 3 * H]
        gcn_w = sb("gcn_w", [H, H], fp32)
        gcn_b_all = sb("gcn_b_all", [P, H], fp32)
        gamma_all = sb("gamma_all", [P, H], fp32)
        beta_all = sb("beta_all", [P, H], fp32)
        self_wT = sb("self_wT", [H, H], fp32)
        neigh_wT = sb("neigh_wT", [H, H], fp32)
        mean_all = sb("mean_all", [P, H], fp32)
        var_all = sb("var_all", [P, H], fp32)
        ln_sum = sb("ln_sum", [P, CH], fp32)
        w_half = sb("w_half", [P, TP], bf16)

        raw = big[:, 0:7 * TP].rearrange("p (a n) -> p a n", a=7)
        raw_i = raw.bitcast(i32)
        raw_src, raw_dst, raw_type, raw_w_e = raw_i[:, 0, :], raw_i[:, 1, :], raw_i[:, 2, :], raw[:, 3, :]
        src_lin, typed_lin, dst_lin = raw[:, 4, :], raw[:, 5, :], raw[:, 6, :]
        featT = big[0:H, :]
        gin_h = big[:, :].rearrange("p (d f) -> p d f", f=HID)
        squares = big[:, 0:NT * H]
        w_parts = big[:, NT * H:NT * H + 3 * TP].rearrange("p (a n) -> p a n", a=3)
        below = h_all[0:NT, :, :].rearrange("p d f -> p (d f)")[:, 0:TP]
        ring_stage = ring[:, 0:2 * CH * 3 * H].rearrange("p (b d f) -> p b d f", b=2, d=CH)

        ps_agg, ps_count, ps_T, ps_gates = bank("ps_agg"), bank("ps_count"), bank("ps_T"), bank("ps_gates")
        ps_typed, ps_u, ps_v, ps_T2 = bank("ps_typed"), bank("ps_u"), bank("ps_v"), bank("ps_T2")

        loaded = sem("loaded")
        pads_set = sem("pads_set")
        consts_made = sem("consts_made")
        dve_consts = sem("dve_consts")
        w_turned = sem("w_turned")
        w_copied = sem("w_copied")
        edges_linear = sem("edges_linear")
        edges_turned = sem("edges_turned")
        edges_copied = sem("edges_copied")
        last_dst = sem("last_dst")
        open_counted = sem("open_counted")
        open_turned = sem("open_turned")
        open_ready = sem("open_ready")
        idx_staged = [sem(f"idx_staged{i}") for i in range(2)]
        pool_go = sem("pool_go")
        group_landed = [sem(f"group_landed{i}") for i in range(RING // GROUP)]
        gathered = sem("gathered")
        tile_used = sem("tile_used")
        onehot_ready = sem("onehot_ready")
        agg_ready = sem("agg_ready")
        sum_ready = sem("sum_ready")
        aggT_ready = sem("aggT_ready")
        aggT_copied = sem("aggT_copied")
        hT_cur_ready = sem("hT_cur_ready")
        gates_ready = sem("gates_ready")
        sig_ready = sem("sig_ready")
        cand_ready = sem("cand_ready")
        tanh_ready = sem("tanh_ready")
        row_ready = sem("row_ready")
        rowT_ready = sem("rowT_ready")
        rowT_copied = sem("rowT_copied")
        typed_ready = sem("typed_ready")
        source_ready = sem("source_ready")
        hi_ready = sem("hi_ready")
        rest_ready = sem("rest_ready")
        mid_ready = sem("mid_ready")
        lo_ready = sem("lo_ready")
        table_written = sem("table_written")
        u_ready = sem("u_ready")
        u_copied = sem("u_copied")
        v_ready = sem("v_ready")
        v_copied = sem("v_copied")
        var_ready = sem("var_ready")
        std_ready = sem("std_ready")
        o_ready = sem("o_ready")
        o_biased = sem("o_biased")
        relu_done = sem("relu_done")
        deg_ready = sem("deg_ready")
        deg_root = sem("deg_root")
        bn_masked = sem("bn_masked")
        bn_mean = sem("bn_mean")
        bn_centred = sem("bn_centred")
        bn_squared = sem("bn_squared")
        bn_var = sem("bn_var")
        bn_var_copied = sem("bn_var_copied")
        bn_std = sem("bn_std")
        ch_centred = sem("ch_centred")
        ch_squared = sem("ch_squared")
        ch_var = sem("ch_var")
        ch_std = sem("ch_std")
        ch_done = sem("ch_done")
        ch_hi = sem("ch_hi")
        ch_rest = sem("ch_rest")
        ch_mid = sem("ch_mid")
        ch_lo = sem("ch_lo")
        sage_written = [sem(f"sage_written{i}") for i in range(2)]
        x_cur_ready = sem("x_cur_ready")
        xT_ready = sem("xT_ready")
        xT_copied = sem("xT_copied")
        out_ready = sem("out_ready")
        out_written = sem("out_written")

        block = ctx.enter_context(nc.Block())

        EDGE_ROWS = E // TP
        EDGE_REST = E - EDGE_ROWS * TP
        LOADS = 4 * 3 + 2 + 25
        ALL_LOADED = 16 * LOADS

        @block.sync
        def _(sp):
            sp.wait_ge(pads_set, 2)
            for a, t in ((0, src), (1, dst), (2, edge_type), (3, edge_weight)):
                to = raw[:, 3, :] if a == 3 else raw_i[:, a, :]
                for r0, r1 in ((0, 112), (112, EDGE_ROWS)):
                    sp.dma_start(to[r0:r1, :], t[r0 * TP:r1 * TP].rearrange("(p n) -> p n", n=TP)
                                 ).then_inc(loaded, 16)
                sp.dma_start(to[EDGE_ROWS:EDGE_ROWS + 1, 0:EDGE_REST],
                             t[EDGE_ROWS * TP:E].rearrange("(p n) -> p n", p=1)).then_inc(loaded, 16)
            sp.dma_start(x_all[:, 0:NT - 1, :],
                         x[0:(NT - 1) * P, :].rearrange("(d p) f -> p d f", p=P)).then_inc(loaded, 16)
            sp.dma_start(x_all[0:LAST, NT - 1, :], x[(NT - 1) * P:N, :]).then_inc(loaded, 16)

            sp.wait_ge(edges_copied, TR)
            for p in range(PASSES):
                idx = typed_idx if p < STEPS else src_idx

                def stage_block(b, half):
                    sp.dma_start(idx_stage[:, half, :], idx[:, ds(b * BLOCK, BLOCK)]
                                 ).then_inc(idx_staged[half], 16)

                def relay(i, g):
                    sp.wait_ge(group_landed[g], (i + 1 + ROUNDS * p) * 16 * GROUP)
                    sp.sem_inc(gathered, GROUP)

                stage_block(0, 0)
                stage_block(1, 1)
                half = RING // GROUP // 2
                with sp.Fori(0, ROUNDS - 1) as i:
                    for g in range(half):
                        relay(i, g)
                    stage_block(i * 2 + 2, 0)
                    for g in range(half, 2 * half):
                        relay(i, g)
                    stage_block(i * 2 + 3, 1)
                for g in range(2 * half):
                    relay(ROUNDS - 1, g)

        @block.gpsimd
        def _(pool):
            nc.gpsimd.memset(raw_i[:, 0, :], 0)
            nc.gpsimd.memset(raw_i[:, 1, :], NO_NODE)
            nc.gpsimd.memset(raw_i[:, 2, :], 0)
            nc.gpsimd.memset(raw[:, 3, :], 0.0).then_inc(pads_set, 1)
            nc.gpsimd.memset(x_all[:, NT - 1, :], 0.0).then_inc(pads_set, 1)
            nc.gpsimd.iota(iota_row[:, :], pattern=[[1, P]], base=0, channel_multiplier=0,
                           allow_small_or_imprecise_dtypes=True)
            nc.gpsimd.iota(iota_col[:, :], pattern=[[0, 1]], base=0, channel_multiplier=1,
                           allow_small_or_imprecise_dtypes=True)
            nc.gpsimd.iota(bound_col[:, :], pattern=[[0, 1]], base=P, channel_multiplier=P,
                           allow_small_or_imprecise_dtypes=True)
            nc.gpsimd.memset(zeros[:, :], 0.0)
            nc.gpsimd.memset(ones_bf[:, :], 1.0)
            nc.gpsimd.memset(ones_row[:, :], 1.0)
            nc.gpsimd.memset(ones_mean[:, :], 1.0 / N)
            nc.gpsimd.memset(eps_col[:, :], EPS)
            nc.gpsimd.memset(first_open[:, 0:1], 0)
            nc.gpsimd.memset(gate_in_w[:, 3 * H:4 * H], 0.0)
            nc.gpsimd.memset(gate_h_w[:, 2 * H:3 * H], 0.0)
            nc.gpsimd.memset(agg_sum[:, :], 0.0)
            nc.gpsimd.memset(row_new[:, :], 0.0)
            pool.drain()
            for t in (aggT, hT_cur, hT_new):
                nc.gpsimd.memset(t[H:H + 1, :], 1.0)
            pool.drain().then_inc(consts_made, 1)

            for p in range(PASSES):
                F3 = 3 * width(p)
                slots = RING * H // width(p)
                if p < SAGE:
                    pool.wait_ge(table_written, 16 * NT * (p + 1))
                else:
                    for i in range(2):
                        pool.wait_ge(sage_written[i], 16 * len(range(i, NCH, 2)))
                pool.sem_inc(pool_go, 1)
                with pool.Fori(0, ROUNDS) as i:
                    for t in range(RING):
                        if t % BLOCK == 0:
                            pool.wait_ge(idx_staged[t // BLOCK], (i + 1 + ROUNDS * p) * 16)
                            pool.sem_inc(pool_go, 1)
                        if t % GROUP == 0:
                            pool.wait_ge(tile_used, i * RING + (FULL * p + t + GROUP + RING - slots))
                            pool.sem_inc(pool_go, 1)
                        s = t % slots
                        pool.indirect_dma_start(
                            out=ring[:, s * F3:(s + 1) * F3], out_offset=None, in_=tables[p].ap(),
                            in_offset=bass.IndirectOffsetOnAxis(
                                ap=idx_stage[:, t // BLOCK, t % BLOCK:t % BLOCK + 1], axis=0)
                        ).then_inc(group_landed[t // GROUP], 16)

        @block.tensor
        def _(pe):
            pe.wait_ge(loaded, ALL_LOADED)
            pe.wait_ge(dve_consts, 1)
            nc.tensor.transpose(ps_T[0:H, 0:P], raw_w[:, 0, :], ident[:, :])
            nc.tensor.transpose(ps_T[0:H, P:2 * P], raw_w[:, 1, :], ident[:, :])
            nc.tensor.transpose(ps_T[0:H, 2 * P:3 * P], raw_w[:, 2, :], ident[:, :])
            nc.tensor.transpose(ps_T[0:H, 3 * P:3 * P + H], raw_w[0:H, 3, :], ident[0:H, 0:H])
            nc.tensor.transpose(ps_gates[0:H, 0:P], raw_w[:, 4, :], ident[:, :])
            nc.tensor.transpose(ps_gates[0:H, P:P + H], raw_w[0:H, 5, :], ident[0:H, 0:H])
            nc.tensor.transpose(ps_gates[0:H, 2 * P:2 * P + H], raw_w[0:H, 6, :], ident[0:H, 0:H])
            nc.tensor.transpose(ps_gates[0:H, 3 * P:3 * P + H], raw_w[0:H, 7, :], ident[0:H, 0:H]
                                ).then_inc(w_turned, 1)
            pe.wait_ge(edges_linear, 1)
            turn = [ps_u, ps_v]
            for j in range(TR):
                if j >= 2:
                    pe.wait_ge(edges_copied, j - 1)
                for a, t in enumerate((src_lin, typed_lin, dst_lin, raw_w_e)):
                    last = nc.tensor.transpose(turn[j % 2][:, a * P:(a + 1) * P], t[:, j * P:(j + 1) * P],
                                               ident[:, :])
                last.then_inc(edges_turned, 1)
            pe.wait_ge(edges_copied, TR)
            q = TP // 4
            for c, b in enumerate((ps_u, ps_v, ps_typed, ps_T2)):
                last = nc.tensor.matmul(b[0:NT, 0:q], pick_last[:, :], dst_f[:, c * q:(c + 1) * q],
                                        start=True, stop=True)
            last.then_inc(last_dst, 1)
            pe.wait_ge(open_counted, 1)
            nc.tensor.matmul(ps_count[0:1, 0:NT], open_col[0:NT, :], ident[0:NT, 0:NT],
                             start=True, stop=True).then_inc(open_turned, 1)
            pe.wait_ge(w_copied, 1)

            def typed_rows(p, d):
                pe.wait_ge(row_ready, NT * (p + 1) + 1 + d)
                nc.tensor.transpose(ps_T2[:, 0:P], row_new[:, :], ident[:, :]).then_inc(rowT_ready, 1)
                pe.wait_ge(rowT_copied, NT * (p + 1) + 1 + d)
                nc.tensor.matmul(ps_typed[:, 0:K * H], hT_new[:, :], typed_w[:, :],
                                 start=True, stop=True).then_inc(typed_ready, 1)

            with pe.Fori(0, NT) as d:
                typed_rows(-1, d)
            pe.wait_ge(open_ready, 1)

            for p in range(PASSES):
                F3 = 3 * width(p)
                slots = RING * H // width(p)
                parts = 3 if p == SAGE else 1

                def tile_product(onehots, t, last):
                    rows_t = ring[:, ds((t % slots) * F3, F3)]
                    for a in range(parts):
                        oh = onehots[:, a * P:(a + 1) * P] if isinstance(onehots, bass.AP) else onehots(a)
                        if p == 0:
                            nc.tensor.matmul(ps_count[:, 0:1], oh, ones_bf[:, :], start=False, stop=last)
                        ins = nc.tensor.matmul(ps_agg[:, 0:F3], oh, rows_t, start=False,
                                               stop=last and a == parts - 1)
                    return ins

                def node_tile(d):
                    lo = pe.value_load(first_open[0:1, ds(d, 1)], min_val=0, max_val=FULL)
                    hi = pe.value_load(first_open[0:1, ds(d + 1, 1)], min_val=0, max_val=FULL)
                    nc.tensor.matmul(ps_agg[:, 0:F3], zeros[:, 0:P], zeros[:, 0:F3], start=True, stop=False)
                    if p == 0:
                        nc.tensor.matmul(ps_count[:, 0:1], zeros[:, 0:P], zeros[:, 0:1], start=True, stop=False)
                    with pe.If(lo < hi):
                        with pe.Fori(lo, hi) as t:
                            pe.wait_ge(onehot_ready, t + d + (1 + (FULL + NT) * p))
                            pe.wait_ge(gathered, t + (1 + TP * p))
                            slot = (t % OHS) * 3 * P
                            flat = onehot[:, :, :].rearrange("p s n -> p (s n)")
                            tile_product(lambda a: flat[:, ds(slot + a * P, P)], t, False
                                         ).then_inc(tile_used, 1)
                    pe.wait_ge(onehot_ready, hi + d + (1 + (FULL + NT) * p))
                    pe.wait_ge(gathered, hi + (1 + TP * p))
                    tile_product(lambda a: onehot_edge[:, a * P:(a + 1) * P], hi, True).then_inc(agg_ready, 1)
                    here = NT * p + 1
                    if p == SAGE:
                        pe.wait_ge(x_cur_ready, d + 1)
                        nc.tensor.transpose(ps_T2[:, 0:P], row_new[:, :], ident[:, :]).then_inc(xT_ready, 1)
                    pe.wait_ge(sum_ready, here + d)
                    nc.tensor.transpose(ps_T[:, 0:P], agg_sum[:, :], ident[:, :]).then_inc(aggT_ready, 1)
                    if p < STEPS:
                        pe.wait_ge(hT_cur_ready, here + d)
                        nc.tensor.matmul(ps_gates[:, 0:4 * H], hT_cur[:, :], gate_h_w[:, :],
                                         start=True, stop=False)
                        pe.wait_ge(aggT_copied, here + d)
                        nc.tensor.matmul(ps_gates[:, 0:4 * H], aggT[:, :], gate_in_w[:, :],
                                         start=False, stop=True).then_inc(gates_ready, 1)
                        if p < STEPS - 1:
                            typed_rows(p, d)
                    elif p in (GIN1, GIN2):
                        base = NT * (p - GIN1) + 1
                        pe.wait_ge(aggT_copied, here + d)
                        if p == GIN1:
                            nc.tensor.matmul(ps_u[:, 0:P], w1a[:, :], aggT[0:H, :],
                                             start=True, stop=True).then_inc(u_ready, 1)
                        else:
                            nc.tensor.matmul(ps_u[:, 0:P], w2a[:, :], aggT_wide[:, :],
                                             start=True, stop=True).then_inc(u_ready, 1)
                        pe.wait_ge(u_copied, base + d)
                        O = HID if p == GIN1 else H
                        nc.tensor.matmul(ps_v[:, 0:O], uT[:, :], (w1b if p == GIN1 else w2b)[:, :],
                                         start=True, stop=False)
                        nc.tensor.matmul(ps_v[:, 0:O], ones_row[:, :], b1b_row if p == GIN1 else b2b_row,
                                         start=False, stop=True).then_inc(v_ready, 1)
                    elif p == GCN:
                        pe.wait_ge(aggT_copied, here + d)
                        nc.tensor.matmul(ps_u[:, 0:H], aggT[0:H, :], gcn_w[:, :],
                                         start=True, stop=True).then_inc(o_ready, 1)
                    else:
                        pe.wait_ge(xT_copied, d + 1)
                        nc.tensor.matmul(ps_v[:, 0:H], hT_new[0:H, :], self_wT[:, :], start=True, stop=False)
                        nc.tensor.matmul(ps_v[:, 0:H], ones_row[:, :], b_self_row, start=False, stop=False)
                        nc.tensor.matmul(ps_v[:, 0:H], ones_row[:, :], b_neigh_row, start=False, stop=True)
                        pe.wait_ge(aggT_copied, here + d)
                        nc.tensor.matmul(ps_u[:, 0:H], aggT[0:H, :], neigh_wT[:, :],
                                         start=True, stop=True).then_inc(o_ready, 1)

                if p < SAGE:
                    with pe.Fori(0, NT) as d:
                        node_tile(d)
                else:
                    with pe.Fori(0, NT - 1) as d:
                        node_tile(d)
                    node_tile(NT - 1)

                if p == GCN:
                    h_flat = h_all[:, :, :].rearrange("p d f -> p (d f)")
                    for ready, data, bk, done in ((bn_masked, h_flat, ps_v, bn_mean),
                                                  (bn_squared, squares, ps_u, bn_var)):
                        pe.wait_ge(ready, 1)
                        for c in range(0, NT * H, 512):
                            n = min(512, NT * H - c)
                            last = nc.tensor.matmul(bk[:, 0:n], ones_mean[:, :], data[:, c:c + n],
                                                    start=c == 0, stop=c + 512 >= NT * H)
                        last.then_inc(done, 1)

        @block.scalar
        def _(act):
            pieces = [
                (raw_w[:, 0:2, :], g_W.rearrange("(c k) h d -> (k h) c d", c=2)),
                (raw_w[:, 2, :], g_w_ih[0:P, :]), (raw_w[0:H, 3, :], g_w_ih[P:3 * H, :]),
                (raw_w[:, 4, :], g_w_hh[0:P, :]), (raw_w[0:H, 5, :], g_w_hh[P:3 * H, :]),
                (raw_w[0:H, 6, :], W_self), (raw_w[0:H, 7, :], W_neigh),
                (typed_w[H:H + 1, :], g_b.rearrange("(o k) h -> o (k h)", o=1)),
                (gate_in_w[H:H + 1, 0:3 * H], g_b_ih.rearrange("(o n) -> o n", o=1)),
                (gate_h_w[H:H + 1, 0:2 * H], g_b_hh[0:2 * H].rearrange("(o n) -> o n", o=1)),
                (gate_h_w[H:H + 1, 3 * H:4 * H], g_b_hh[2 * H:3 * H].rearrange("(o n) -> o n", o=1)),
                (w1a[:, :], W1a), (w1b[:, :], W1b), (w2a[:, :], W2a), (w2b[:, :], W2b),
                (b1a_col[:, :], b1a.rearrange("(n o) -> n o", o=1)),
                (b2a_col[:, :], b2a.rearrange("(n o) -> n o", o=1)),
                (rows[0:1, 0:HID], b1b.rearrange("(o n) -> o n", o=1)),
                (rows[0:1, HID:HID + H], b2b.rearrange("(o n) -> o n", o=1)),
                (rows[0:1, HID + H:HID + 2 * H], b_self.rearrange("(o n) -> o n", o=1)),
                (rows[0:1, HID + 2 * H:HID + 3 * H], b_neigh.rearrange("(o n) -> o n", o=1)),
                (gcn_w[:, :], gcn_W),
            ]
            act.wait_ge(consts_made, 1)
            for to, frm in pieces:
                act.dma_start(to, frm).then_inc(loaded, 16)
            for to, frm in ((gcn_b_all, gcn_b), (gamma_all, gamma), (beta_all, beta)):
                act.dma_start(to[:, :], frm.rearrange("(o n) -> o n", o=1).to_broadcast([P, H])
                              ).then_inc(loaded, 16)
            assert len(pieces) + 3 + 12 + 2 == LOADS, len(pieces)

            def split_and_store(p, d, source, groups, W, table_rows):
                at = NT * (p + 1) + d
                hi, mid = stage_parts(groups, W)[0:2]
                if not (isinstance(at, int) and at == 0):
                    act.wait_ge(table_written, at * 16)
                act.activation(hi, source, ACT.Copy).then_inc(hi_ready, 1)
                act.wait_ge(rest_ready, at + 1)
                act.activation(mid, rest[:, 0:groups * W].rearrange("p (k w) -> p k w", k=groups), ACT.Copy
                               ).then_inc(mid_ready, 1)
                act.wait_ge(lo_ready, at + 1)
                act.dma_start(table_rows, stage_flat[:, 0:3 * W * groups]).then_inc(table_written, 16)

            stage_flat = stage[:, :, :].rearrange("p k n -> p (k n)")

            def stage_parts(groups, W):
                v = stage_flat[:, 0:3 * W * groups].rearrange("p (k a w) -> p k a w", k=groups, a=3)
                return [v[:, :, a, :] for a in range(3)]

            def typed_rows(p, d):
                at = NT * (p + 1) + 1
                act.wait_ge(rowT_ready, at + d)
                act.activation(hT_new[0:H, :], ps_T2[0:H, 0:P], ACT.Copy).then_inc(rowT_copied, 1)
                act.activation(featT[:, ds(d * P, P)], ps_T2[0:H, 0:P], ACT.Copy)
                act.wait_ge(typed_ready, at + d)
                to = typed[(p + 1) % 2].ap().rearrange("(n k) f -> n (k f)", k=K)[ds(d * P, P), :]
                split_and_store(p, d, ps_typed[:, 0:K * H].rearrange("p (k w) -> p k w", k=K), K, H, to)

            act.wait_ge(edges_copied, TR)
            typed_rows(-1, 0)
            with act.Fori(1, NT) as d:
                typed_rows(-1, d)

            def layernorm_root(k, d):
                act.wait_ge(var_ready, NT * k + 1 + d)
                act.activation(std[:, 0:1], moments[:, 1:2], ACT.Sqrt, bias=eps_col[:, :]).then_inc(std_ready, 1)

            for p in range(PASSES):
                here = NT * p + 1
                if p == 1:
                    act.wait_ge(deg_ready, 1)
                    act.activation(deg_rsqrt[:, :], std[:, :], ACT.Sqrt).then_inc(deg_root, 1)

                def node_tile(d):
                    if p < STEPS:
                        act.activation(hT_cur[0:H, :], featT[:, ds(d * P, P)], ACT.Copy
                                       ).then_inc(hT_cur_ready, 1)
                    if p == SAGE:
                        act.wait_ge(xT_ready, d + 1)
                        act.activation(hT_new[0:H, :], ps_T2[0:H, 0:P], ACT.Copy).then_inc(xT_copied, 1)
                    act.wait_ge(aggT_ready, here + d)
                    if p == GIN2:
                        act.activation(aggT_wide[:, :], ps_T[:, 0:P], ACT.Copy).then_inc(aggT_copied, 1)
                    else:
                        act.activation(aggT[0:H, :], ps_T[0:H, 0:P], ACT.Copy).then_inc(aggT_copied, 1)
                    if p < STEPS:
                        act.wait_ge(gates_ready, here + d)
                        act.activation(gates[:, :], ps_gates[:, 0:2 * H], ACT.Sigmoid).then_inc(sig_ready, 1)
                        act.wait_ge(cand_ready, here + d)
                        act.activation(cand_act[:, :], cand[:, :], ACT.Tanh).then_inc(tanh_ready, 1)
                        if p < STEPS - 1:
                            typed_rows(p, d)
                        else:
                            layernorm_root(0, d)
                            act.wait_ge(source_ready, d + 1)
                            split_and_store(p, d, row_new[:, 0:H].rearrange("p (k w) -> p k w", k=1), 1, H,
                                            gin1_table.ap()[ds(d * P, P), :])
                    elif p in (GIN1, GIN2):
                        base = NT * (p - GIN1) + 1
                        act.wait_ge(u_ready, base + d)
                        act.activation(uT[:, :], ps_u[:, 0:P], ACT.Relu,
                                       bias=(b1a_col if p == GIN1 else b2a_col)[:, :]).then_inc(u_copied, 1)
                        act.wait_ge(v_ready, base + d)
                        if p == GIN1:
                            act.activation(row_new[:, :], ps_v[:, 0:HID], ACT.Relu).then_inc(v_copied, 1)
                            act.drain()
                            split_and_store(p, d, row_new[:, :].rearrange("p (k w) -> p k w", k=1), 1, HID,
                                            gin2_table.ap()[ds(d * P, P), :])
                        else:
                            act.activation(v_row[:, :], ps_v[:, 0:H], ACT.Relu).then_inc(v_copied, 1)
                            layernorm_root(1, d)
                            act.wait_ge(source_ready, NT + 1 + d)
                            split_and_store(p, d, row_new[:, 0:H].rearrange("p (k w) -> p k w", k=1), 1, H,
                                            gcn_table.ap()[ds(d * P, P), :])
                    elif p == GCN:
                        act.wait_ge(o_biased, d + 1)
                        act.activation(h_all[:, ds(d, 1), :].rearrange("p o f -> p (o f)"), o_row[:, :], ACT.Relu
                                       ).then_inc(relu_done, 1)
                    else:
                        layernorm_root(2, d)
                        act.wait_ge(out_ready, d + 1)
                        if isinstance(d, int):
                            act.dma_start(out[d * P:N, :], out_row[0:LAST, :]).then_inc(out_written, 16)
                        else:
                            act.dma_start(out[ds(d * P, P), :], out_row[:, :]).then_inc(out_written, 16)
                        act.wait_ge(out_written, d * 16 + 16)

                if p < SAGE:
                    with act.Fori(0, NT) as d:
                        node_tile(d)
                else:
                    with act.Fori(0, NT - 1) as d:
                        node_tile(d)
                    node_tile(NT - 1)
                    act.wait_ge(out_written, 16 * NT)

                if p == GCN:
                    h_flat = h_all[:, :, :].rearrange("p d f -> p (d f)")
                    act.wait_ge(bn_centred, 1)
                    act.activation(squares, h_flat, ACT.Square).then_inc(bn_squared, 1)
                    act.wait_ge(bn_var_copied, 1)
                    act.activation(var_all[:, :], var_all[:, :], ACT.Sqrt, bias=eps_col[:, :]).then_inc(bn_std, 1)
                    for c in range(NCH):
                        hc = h_all[:, c * CH:(c + 1) * CH, :]
                        sq = squares.rearrange("p (d f) -> p d f", f=H)[:, c * CH:(c + 1) * CH, :]
                        xc = x_all[:, c * CH:(c + 1) * CH, :]
                        st = ring_stage[:, c % 2]
                        act.wait_ge(ch_centred, c + 1)
                        act.activation(sq, hc, ACT.Square).then_inc(ch_squared, 1)
                        act.wait_ge(ch_var, c + 1)
                        act.activation(std[:, 0:CH], ln_sum[:, :], ACT.Sqrt, bias=eps_col[:, :], scale=1.0 / H
                                       ).then_inc(ch_std, 1)
                        act.wait_ge(ch_done, c + 1)
                        if c >= 2:
                            act.wait_ge(sage_written[c % 2], 16 * (c // 2))
                        act.activation(st[:, :, 0:H], xc, ACT.Copy).then_inc(ch_hi, 1)
                        act.wait_ge(ch_rest, c + 1)
                        act.activation(st[:, :, H:2 * H], sq, ACT.Copy).then_inc(ch_mid, 1)
                        act.wait_ge(ch_lo, c + 1)
                        act.dma_start(sage_table.ap()[c * CH * P:(c + 1) * CH * P, :]
                                      .rearrange("(d p) f -> p d f", p=P), st).then_inc(sage_written[c % 2], 16)

        @block.vector
        def _(dve):
            dve.sem_inc(tile_used, RING)
            dve.wait_ge(consts_made, 1)
            v = nc.vector
            v.tensor_scalar(ident[:, :], iota_row[:, :], iota_col[:, :], None, ALU.is_equal)
            v.tensor_scalar(pick_last[:, :], iota_col[:, :].to_broadcast([P, NT]), float(P - 1), None, ALU.is_equal)
            v.tensor_scalar(mask_last[:, :], iota_col[:, :], float(LAST), None, ALU.is_lt)
            dve.drain().then_inc(dve_consts, 1)
            dve.wait_ge(loaded, ALL_LOADED)
            v.scalar_tensor_tensor(out=typed_lin, in0=raw_src, scalar=float(K), in1=raw_type, op0=ALU.mult, op1=ALU.add)
            v.tensor_copy(src_lin, raw_src)
            v.tensor_copy(dst_lin, raw_dst).then_inc(edges_linear, 1)
            dve.wait_ge(w_turned, 1)
            v.tensor_copy(typed_w[0:H, :], ps_T[0:H, 0:2 * P])
            v.tensor_copy(gate_in_w[0:H, 0:3 * H], ps_T[0:H, 2 * P:2 * P + 3 * H])
            v.tensor_copy(gate_h_w[0:H, 0:2 * H], ps_gates[0:H, 0:2 * H])
            v.tensor_copy(gate_h_w[0:H, 3 * H:4 * H], ps_gates[0:H, 2 * H:3 * H])
            v.tensor_copy(self_wT[:, :], ps_gates[0:H, 2 * P:2 * P + H])
            v.tensor_copy(neigh_wT[:, :], ps_gates[0:H, 3 * P:3 * P + H]).then_inc(w_copied, 1)
            turn = [ps_u, ps_v]
            for j in range(TR):
                dve.wait_ge(edges_turned, j + 1)
                for a, to in enumerate((src_idx, typed_idx, dst_f, w_f)):
                    last = v.tensor_copy(to[:, :].rearrange("e (p j) -> e j p", j=TR)[:, j, :],
                                         turn[j % 2][:, a * P:(a + 1) * P])
                last.then_inc(edges_copied, 1)
            dve.wait_ge(last_dst, 1)
            q = TP // 4
            for c, b in enumerate((ps_u, ps_v, ps_typed, ps_T2)):
                v.tensor_scalar(below[:, c * q:(c + 1) * q], b[0:NT, 0:q], bound_col[0:NT, :], None, ALU.is_lt)
            dve.drain()
            v.reduce_sum(open_col[0:NT, :], below, axis=AX.X).then_inc(open_counted, 1)
            dve.wait_ge(open_turned, 1)
            v.tensor_copy(first_open[0:1, 1:NT + 1], ps_count[0:1, 0:NT]).then_inc(open_ready, 1)
            dve.wait_ge(open_ready, 1)

            stage_flat = stage[:, :, :].rearrange("p k n -> p (k n)")

            def split(p, d, source, groups, W):
                at = NT * (p + 1) + 1
                parts = stage_flat[:, 0:3 * W * groups].rearrange("p (k a w) -> p k a w", k=groups, a=3)
                r = rest[:, 0:groups * W].rearrange("p (k w) -> p k w", k=groups)
                dve.wait_ge(hi_ready, at + d)
                v.tensor_tensor(r, source, parts[:, :, 0, :], ALU.subtract).then_inc(rest_ready, 1)
                dve.wait_ge(mid_ready, at + d)
                v.tensor_tensor(parts[:, :, 2, :], r, parts[:, :, 1, :], ALU.subtract).then_inc(lo_ready, 1)

            def typed_rows(p, d):
                split(p, d, ps_typed[:, 0:K * H].rearrange("p (k w) -> p k w", k=K), K, H)

            def tile(t, d):
                return t[:, ds(d, 1), :].rearrange("p o f -> p (o f)")

            def first_state(d):
                v.tensor_copy(row_new[:, 0:H], tile(x_all, d)).then_inc(row_ready, 1)
                v.tensor_copy(tile(h_all, d), tile(x_all, d))
                typed_rows(-1, d)

            with dve.Fori(0, NT) as d:
                first_state(d)

            def layernorm(k, d, to):
                dve.drain()
                v.bn_stats(stats6[:, :], y_row[:, :])
                dve.drain()
                v.bn_aggr(moments[:, :], stats6[:, :]).then_inc(var_ready, 1)
                dve.wait_ge(std_ready, NT * k + 1 + d)
                v.reciprocal(rstd[:, :], std[:, 0:1])
                dve.drain()
                return v.tensor_scalar(to, y_row[:, :], moments[:, 0:1], rstd[:, :], ALU.subtract, ALU.mult)

            for p in range(PASSES):
                W = width(p)
                if p == 1:
                    v.tensor_scalar(inv_count[:, :], count[:, :], 1.0, None, ALU.max)
                    v.tensor_scalar(std[:, :], count[:, :], 1.0, 1.0, ALU.add, ALU.max).then_inc(deg_ready, 1)
                    dve.drain()
                    v.reciprocal(inv_count[:, :], inv_count[:, :])
                    dve.wait_ge(deg_root, 1)
                    v.reciprocal(deg_rsqrt[:, :], deg_rsqrt[:, :])
                if p == GCN:
                    dve.drain()
                    left = w_parts[:, 2, :]
                    v.tensor_copy(left, w_f[:, :])
                    dve.drain()
                    for a in range(2):
                        v.tensor_copy(w_half[:, :], left)
                        dve.drain()
                        v.tensor_copy(w_parts[:, a, :], w_half[:, :])
                        dve.drain()
                        v.tensor_tensor(left, left, w_parts[:, a, :], ALU.subtract)
                        dve.drain()
                v.tensor_scalar(node_ids[:, :], iota_row[:, :], float(P), None, ALU.subtract)
                dve.drain()

                def make_onehot(to, t):
                    if p < SAGE:
                        return v.tensor_scalar(to(0), node_ids[:, :], dst_f[:, ds(t, 1)], None, ALU.is_equal)
                    for a in range(3):
                        last = v.tensor_scalar(to(a), node_ids[:, :], dst_f[:, ds(t, 1)],
                                               w_parts[:, a, :][:, ds(t, 1)], ALU.is_equal, ALU.mult)
                    return last

                def node_tile(d):
                    lo = dve.value_load(first_open[0:1, ds(d, 1)], min_val=0, max_val=FULL)
                    hi = dve.value_load(first_open[0:1, ds(d + 1, 1)], min_val=0, max_val=FULL)
                    v.tensor_scalar(node_ids[:, :], node_ids[:, :], float(P), None, ALU.add)
                    if p == SAGE:
                        v.tensor_copy(row_new[:, 0:H], tile(x_all, d)).then_inc(x_cur_ready, 1)
                    dve.drain()
                    flat = onehot[:, :, :].rearrange("p s n -> p (s n)")
                    with dve.If(lo < hi):
                        with dve.Fori(lo, hi) as t:
                            dve.wait_ge(tile_used, t + (FULL * p + RING - OHS + 1))
                            slot = (t % OHS) * 3 * P
                            make_onehot(lambda a: flat[:, ds(slot + a * P, P)], t).then_inc(onehot_ready, 1)
                    make_onehot(lambda a: onehot_edge[:, a * P:(a + 1) * P], hi).then_inc(onehot_ready, 1)

                    here = NT * p + 1
                    dve.wait_ge(agg_ready, here + d)
                    if p == 0:
                        v.tensor_copy(count[:, ds(d, 1)], ps_count[:, 0:1])
                    v.tensor_copy(agg_sum[:, 0:W], ps_agg[:, 2 * W:3 * W])
                    dve.drain()
                    v.tensor_tensor(agg_sum[:, 0:W], ps_agg[:, W:2 * W], agg_sum[:, 0:W], ALU.add)
                    dve.drain()
                    last = v.tensor_tensor(agg_sum[:, 0:W], ps_agg[:, 0:W], agg_sum[:, 0:W], ALU.add)
                    if p in (GIN1, GIN2):
                        dve.drain()
                        last = v.tensor_tensor(agg_sum[:, 0:W], agg_sum[:, 0:W],
                                               tile(x_all if p == GIN1 else gin_h, d), ALU.add)
                    if p == GCN:
                        dve.drain()
                        last = v.scalar_tensor_tensor(out=agg_sum[:, 0:H], in0=tile(x_all, d),
                                                      scalar=deg_rsqrt[:, ds(d, 1)], in1=agg_sum[:, 0:H],
                                                      op0=ALU.mult, op1=ALU.add)
                    last.then_inc(sum_ready, 1)

                    if p < STEPS:
                        dve.wait_ge(sig_ready, here + d)
                        v.tensor_tensor(cand[:, :], gates[:, 0:H], ps_gates[:, 3 * H:4 * H], ALU.mult)
                        dve.drain()
                        v.tensor_tensor(cand[:, :], cand[:, :], ps_gates[:, 2 * H:3 * H], ALU.add
                                        ).then_inc(cand_ready, 1)
                        dve.wait_ge(tanh_ready, here + d)
                        v.tensor_tensor(diff[:, :], tile(h_all, d), cand_act[:, :], ALU.subtract)
                        dve.drain()
                        v.tensor_tensor(diff[:, :], gates[:, H:2 * H], diff[:, :], ALU.mult)
                        dve.drain()
                        if p < STEPS - 1:
                            v.tensor_tensor(row_new[:, 0:H], cand_act[:, :], diff[:, :], ALU.add
                                            ).then_inc(row_ready, 1)
                            dve.drain()
                            v.tensor_copy(tile(h_all, d), row_new[:, 0:H])
                            typed_rows(p, d)
                        else:
                            v.tensor_tensor(y_row[:, :], cand_act[:, :], diff[:, :], ALU.add)
                            dve.drain()
                            v.tensor_tensor(y_row[:, :], y_row[:, :], tile(x_all, d), ALU.add)
                            layernorm(0, d, row_new[:, 0:H]).then_inc(source_ready, 1)
                            dve.drain()
                            v.tensor_copy(tile(x_all, d), row_new[:, 0:H])
                            split(p, d, row_new[:, 0:H].rearrange("p (k w) -> p k w", k=1), 1, H)
                    elif p == GIN1:
                        dve.wait_ge(v_copied, d + 1)
                        v.tensor_copy(tile(gin_h, d), row_new[:, :])
                        split(p, d, row_new[:, :].rearrange("p (k w) -> p k w", k=1), 1, HID)
                    elif p == GIN2:
                        dve.wait_ge(v_copied, NT + 1 + d)
                        v.tensor_tensor(y_row[:, :], v_row[:, :], tile(x_all, d), ALU.add)
                        layernorm(1, d, o_row[:, :])
                        dve.drain()
                        v.tensor_copy(tile(x_all, d), o_row[:, :])
                        v.tensor_scalar(row_new[:, 0:H], o_row[:, :], deg_rsqrt[:, ds(d, 1)], None, ALU.mult
                                        ).then_inc(source_ready, 1)
                        dve.drain()
                        split(p, d, row_new[:, 0:H].rearrange("p (k w) -> p k w", k=1), 1, H)
                    elif p == GCN:
                        dve.wait_ge(o_ready, d + 1)
                        v.scalar_tensor_tensor(out=o_row[:, :], in0=ps_u[:, 0:H], scalar=deg_rsqrt[:, ds(d, 1)],
                                               in1=gcn_b_all[:, :], op0=ALU.mult, op1=ALU.add
                                               ).then_inc(o_biased, 1)
                        dve.wait_ge(relu_done, d + 1)
                    else:
                        dve.wait_ge(o_ready, NT + 1 + d)
                        v.tensor_copy(o_row[:, :], ps_v[:, 0:H])
                        dve.drain()
                        v.scalar_tensor_tensor(out=y_row[:, :], in0=ps_u[:, 0:H], scalar=inv_count[:, ds(d, 1)],
                                               in1=o_row[:, :], op0=ALU.mult, op1=ALU.add)
                        dve.drain()
                        v.tensor_tensor(y_row[:, :], y_row[:, :], tile(x_all, d), ALU.add)
                        layernorm(2, d, out_row[:, :]).then_inc(out_ready, 1)

                if p < SAGE:
                    with dve.Fori(0, NT) as d:
                        node_tile(d)
                else:
                    with dve.Fori(0, NT - 1) as d:
                        node_tile(d)
                    node_tile(NT - 1)

                if p == GCN:
                    def fold(to, bk):
                        return v.tensor_reduce(out=to, in_=bk[:, :].rearrange("p (g c) -> p c g", g=8),
                                               axis=AX.X, op=ALU.add)

                    def over(t, n):
                        return t[:, :].rearrange("p (o f) -> p o f", o=1).to_broadcast([P, n, H])

                    def mask():
                        return v.tensor_scalar(h_all[:, NT - 1, :], h_all[:, NT - 1, :], mask_last[:, :], None,
                                               ALU.mult)

                    mask().then_inc(bn_masked, 1)
                    dve.wait_ge(bn_mean, 1)
                    fold(mean_all[:, :], ps_v)
                    dve.drain()
                    v.tensor_tensor(h_all[:, :, :], h_all[:, :, :], over(mean_all, NT), ALU.subtract)
                    dve.drain()
                    mask().then_inc(bn_centred, 1)
                    dve.wait_ge(bn_var, 1)
                    fold(var_all[:, :], ps_u).then_inc(bn_var_copied, 1)
                    dve.wait_ge(bn_std, 1)
                    v.reciprocal(var_all[:, :], var_all[:, :])
                    dve.drain()
                    v.tensor_tensor(gamma_all[:, :], gamma_all[:, :], var_all[:, :], ALU.mult)
                    dve.drain()
                    for c in range(NCH):
                        hc = h_all[:, c * CH:(c + 1) * CH, :]
                        sq = squares.rearrange("p (d f) -> p d f", f=H)[:, c * CH:(c + 1) * CH, :]
                        xc = x_all[:, c * CH:(c + 1) * CH, :]
                        st = ring_stage[:, c % 2]

                        def per_node(t):
                            return t[:, 0:CH].rearrange("p (d o) -> p d o", o=1).to_broadcast([P, CH, H])

                        v.tensor_tensor(hc, hc, over(gamma_all, CH), ALU.mult)
                        dve.drain()
                        v.tensor_tensor(hc, hc, over(beta_all, CH), ALU.add)
                        dve.drain()
                        v.tensor_tensor(hc, hc, xc, ALU.add)
                        dve.drain()
                        v.reduce_sum(ln_sum[:, :], hc, axis=AX.X)
                        dve.drain()
                        v.tensor_scalar(ln_sum[:, :], ln_sum[:, :], 1.0 / H, None, ALU.mult)
                        dve.drain()
                        v.tensor_tensor(hc, hc, per_node(ln_sum), ALU.subtract).then_inc(ch_centred, 1)
                        dve.wait_ge(ch_squared, c + 1)
                        v.reduce_sum(ln_sum[:, :], sq, axis=AX.X).then_inc(ch_var, 1)
                        dve.wait_ge(ch_std, c + 1)
                        v.reciprocal(ln_sum[:, :], std[:, 0:CH])
                        dve.drain()
                        v.tensor_tensor(xc, hc, per_node(ln_sum), ALU.mult).then_inc(ch_done, 1)
                        dve.wait_ge(ch_hi, c + 1)
                        v.tensor_tensor(sq, xc, st[:, :, 0:H], ALU.subtract).then_inc(ch_rest, 1)
                        dve.wait_ge(ch_mid, c + 1)
                        v.tensor_tensor(st[:, :, 2 * H:3 * H], sq, st[:, :, H:2 * H], ALU.subtract
                                        ).then_inc(ch_lo, 1)


_INS = ['x', 'src', 'dst', 'edge_type_4', 'edge_weight', 'L0_gnn_W', 'L0_gnn_b', 'L0_gnn_w_ih', 'L0_gnn_w_hh',
        'L0_gnn_b_ih', 'L0_gnn_b_hh', 'L1_gnn_W1a', 'L1_gnn_b1a', 'L1_gnn_W1b', 'L1_gnn_b1b', 'L1_gnn_W2a',
        'L1_gnn_b2a', 'L1_gnn_W2b', 'L1_gnn_b2b', 'L2_gnn_W', 'L2_gnn_b', 'L2_gnn_gamma', 'L2_gnn_beta',
        'L3_gnn_W_self', 'L3_gnn_b_self', 'L3_gnn_W_neigh', 'L3_gnn_b_neigh']


def kernel(**inputs):
    import numpy as _np
    import concourse.bacc as _bacc
    from concourse import mybir as _mybir
    from concourse.bass_utils import run_bass_kernel_spmd as _run

    nc = _bacc.Bacc("TRN2", target_bir_lowering=False, num_devices=1)
    arrays, args = {}, []
    for name in _INS:
        a = _np.ascontiguousarray(inputs[name])
        arrays[f"in_{name}"] = a
        args.append(nc.dram_tensor(f"in_{name}", a.shape, _mybir.dt.from_np(a.dtype), kind="ExternalInput").ap())
    out = nc.dram_tensor("out_0", (N, H), _mybir.dt.float32, kind="ExternalOutput").ap()
    build(nc, *args, out)
    r = _run(nc, [arrays], core_ids=[0])
    return r.results[0]["out_0"]
```

```python
import concourse.bass as bass
from concourse import mybir
from contextlib import ExitStack

N = 12500
H = 64
E = 212500
K = 4
HID = 128
P = 128
NT = -(-N // P)
NP = NT * P
LAST = N - (NT - 1) * P
RING = 64
GROUP = 8
BLOCK = 32
TP = -(-E // (P * RING)) * RING
B = 4
FULL = E // (P * B)
TR = TP // P
ROUNDS = TP // RING
OHS = 16
OHS_W = 8
CREDIT = 32
AHEAD = OHS_W
PB = 2
NPB = NT // PB
STEPS = 4
GIN1, GIN2, GCN, SAGE = 4, 5, 6, 7
PASSES = 8
EPS = 1e-5
CH = 14
NCH = NT // CH
NO_NODE = 20000


def build(nc, x, src, dst, edge_type, edge_weight, g_W, g_b, g_w_ih, g_w_hh, g_b_ih, g_b_hh,
          W1a, b1a, W1b, b1b, W2a, b2a, W2b, b2b, gcn_W, gcn_b, gamma, beta,
          W_self, b_self, W_neigh, b_neigh, out):
    fp32, bf16, i32, i16 = mybir.dt.float32, mybir.dt.bfloat16, mybir.dt.int32, mybir.dt.int16
    ALU, ACT, AX = mybir.AluOpType, mybir.ActivationFunctionType, mybir.AxisListType
    ds = bass.ds

    typed = [nc.dram_tensor(f"typed_table{i}", [NP * K, 3 * H], bf16) for i in range(2)]
    gin1_table = nc.dram_tensor("gin1_table", [NP, 3 * H], bf16)
    gin2_table = nc.dram_tensor("gin2_table", [NP, 3 * HID], bf16)
    gcn_table = nc.dram_tensor("gcn_table", [NP, 3 * H], bf16)
    sage_table = nc.dram_tensor("sage_table", [NP, 3 * H], bf16)
    tables = [typed[0], typed[1], typed[0], typed[1], gin1_table, gin2_table, gcn_table, sage_table]

    def width(p):
        return HID if p == GIN2 else H

    ctx = ExitStack()
    with ctx:
        def sb(name, shape, dt):
            return ctx.enter_context(nc.sbuf_tensor(name, shape, dt))

        def bank(name):
            return ctx.enter_context(nc.psum_tensor(name, [P, 512], fp32))

        def sem(name):
            return ctx.enter_context(nc.semaphore(name))

        x_all = sb("x_all", [P, NT, H], fp32)
        h_all = sb("h_all", [P, NT, H], fp32)
        big = sb("big", [P, NT * P], fp32)
        ring = sb("ring", [P, RING * 3 * H], bf16)
        onehot = sb("onehot", [P, max(OHS, 3 * OHS_W) * B * P], bf16)
        onehot_edge = sb("onehot_edge", [P, 3 * B * P], bf16)
        typed_idx = sb("typed_idx", [P, TP], i32)
        src_idx = sb("src_idx", [P, TP], i32)
        dst_id = sb("dst_id", [P, TP], i16)
        w_f = sb("w_f", [P, TP], fp32)
        idx_stage = sb("idx_stage", [P, 2, BLOCK], i32)
        zeros = sb("zeros", [P, 3 * HID], bf16)
        zero_row = sb("zero_row", [P, H], fp32)
        ones_bf = sb("ones_bf", [P, 1], bf16)
        ones_row = sb("ones_row", [1, P], fp32)
        ones_mean = sb("ones_mean", [P, P], fp32)
        eps_col = sb("eps_col", [P, 1], fp32)
        iota_row = sb("iota_row", [P, P], fp32)
        iota_col = sb("iota_col", [P, 1], fp32)
        bound_col = sb("bound_col", [P, 1], fp32)
        ident = sb("ident", [P, P], fp32)
        pick_last = sb("pick_last", [P, NT], fp32)
        mask_last = sb("mask_last", [P, 1], fp32)
        first_ids = sb("first_ids", [P, P, B], i16)
        node_ids = sb("node_ids", [P, P, B], i16)
        matches = sb("matches", [P, P, B], bf16)
        open_col = sb("open_col", [P, 1], fp32)
        first_open = sb("first_open", [1, NT + 2], i32)
        ahead_end = sb("ahead_end", [1, NT + 1], i32)
        count = sb("count", [P, NT], fp32)
        inv_count = sb("inv_count", [P, NT], fp32)
        deg_rsqrt = sb("deg_rsqrt", [P, NT], fp32)
        agg_sum = sb("agg_sum", [P, HID], fp32)
        aggT = sb("aggT", [H + 1, P], fp32)
        aggT_wide = sb("aggT_wide", [P, P], fp32)
        hT_cur = sb("hT_cur", [H + 1, P], fp32)
        hT_new = sb("hT_new", [H + 1, P], fp32)
        gates = sb("gates", [P, 2 * H], fp32)
        cand = sb("cand", [P, H], fp32)
        cand_act = sb("cand_act", [P, H], fp32)
        diff = sb("diff", [P, H], fp32)
        row_new = sb("row_new", [P, HID], fp32)
        y_row = sb("y_row", [P, H], fp32)
        v_row = sb("v_row", [P, H], fp32)
        o_row = sb("o_row", [P, H], fp32)
        out_row = sb("out_row", [P, H], fp32)
        uT = sb("uT", [P, P], fp32)
        rest = sb("rest", [P, K * H], fp32)
        stage = sb("stage", [P, K, 3 * H], bf16)
        stats6 = sb("stats6", [P, nc.vector.BN_STATS_DIM], fp32)
        moments = sb("moments", [P, 2], fp32)
        std = sb("std", [P, NT], fp32)
        rstd = sb("rstd", [P, 1], fp32)
        typed_w = sb("typed_w", [H + 1, K * H], fp32)
        gate_in_w = sb("gate_in_w", [H + 1, 4 * H], fp32)
        gate_h_w = sb("gate_h_w", [H + 1, 4 * H], fp32)
        raw_w = sb("raw_w", [P, 8, H], fp32)
        w1a = sb("w1a", [H, HID], fp32)
        w1b = sb("w1b", [HID, HID], fp32)
        w2a = sb("w2a", [HID, HID], fp32)
        w2b = sb("w2b", [HID, H], fp32)
        b1a_col = sb("b1a_col", [HID, 1], fp32)
        b2a_col = sb("b2a_col", [HID, 1], fp32)
        rows = sb("rows", [1, HID + 3 * H], fp32)
        b1b_row, b2b_row = rows[0:1, 0:HID], rows[0:1, HID:HID + H]
        b_self_row, b_neigh_row = rows[0:1, HID + H:HID + 2 * H], rows[0:1, HID + 2 * H:HID + 3 * H]
        gcn_w = sb("gcn_w", [H, H], fp32)
        gcn_b_all = sb("gcn_b_all", [P, H], fp32)
        gamma_all = sb("gamma_all", [P, H], fp32)
        beta_all = sb("beta_all", [P, H], fp32)
        self_wT = sb("self_wT", [H, H], fp32)
        neigh_wT = sb("neigh_wT", [H, H], fp32)
        mean_all = sb("mean_all", [P, H], fp32)
        var_all = sb("var_all", [P, H], fp32)
        ln_sum = sb("ln_sum", [P, NT], fp32)
        ln_rstd = sb("ln_rstd", [P, NT], fp32)
        mean_last = sb("mean_last", [P, P], fp32)

        raw = big[:, 0:7 * TP].rearrange("p (a n) -> p a n", a=7)
        raw_i = raw.bitcast(i32)
        raw_src, raw_dst, raw_type, raw_w_e = raw_i[:, 0, :], raw_i[:, 1, :], raw_i[:, 2, :], raw[:, 3, :]
        src_lin, typed_lin, dst_lin = raw[:, 4, :], raw[:, 5, :], raw[:, 6, :]
        featT = big[0:H, :]
        gin_h = big[:, :].rearrange("p (d f) -> p d f", f=HID)
        squares = big[:, 0:NT * H]
        w_left = big[:, NT * H:NT * H + TP]
        w_parts = big[:, NT * H + TP:NT * H + TP + 3 * TP // 2].bitcast(bf16).rearrange("p (a n) -> p a n", a=3)
        below = onehot[0:NT, :].bitcast(fp32)[:, 0:TP // B]
        ring_stage = ring[:, 0:4 * CH * 3 * H].rearrange("p (b d f) -> p b d f", b=4, d=CH)
        ring_f = ring[:, :].bitcast(fp32)
        dst_f = ring_f[:, 0:TP]
        first_stage = ring[:, 2 * TP:2 * TP + 2 * PB * K * 3 * H].rearrange("p (b n) -> p b n", b=2)
        at_rest = TP + PB * K * 3 * H
        first_rest = ring_f[:, at_rest:at_rest + 2 * PB * K * H].rearrange("p (b n) -> p b n", b=2)
        at_x = at_rest + 2 * PB * K * H
        first_x = ring_f[:, at_x:at_x + 2 * (PB + 1) * H].rearrange("p (b n) -> p b n", b=2)
        at_T = at_x + 2 * (PB + 1) * H
        firstT = ring_f[0:H + 1, at_T:at_T + 2 * PB * P].rearrange("p (b n) -> p b n", b=2)

        ps_agg, ps_count, ps_T, ps_gates = bank("ps_agg"), bank("ps_count"), bank("ps_T"), bank("ps_gates")
        ps_typed, ps_u, ps_v, ps_T2 = bank("ps_typed"), bank("ps_u"), bank("ps_v"), bank("ps_T2")

        loaded = sem("loaded")
        x_loaded = sem("x_loaded")
        state_loaded = sem("state_loaded")
        pads_set = sem("pads_set")
        consts_made = sem("consts_made")
        dve_consts = sem("dve_consts")
        w_turned = sem("w_turned")
        w_copied = sem("w_copied")
        edges_linear = sem("edges_linear")
        edges_turned = sem("edges_turned")
        edges_copied = sem("edges_copied")
        last_dst = sem("last_dst")
        open_counted = sem("open_counted")
        open_turned = sem("open_turned")
        open_ready = sem("open_ready")
        idx_staged = [sem(f"idx_staged{i}") for i in range(2)]
        pool_go = sem("pool_go")
        dve_go = sem("dve_go")
        group_landed = [sem(f"group_landed{i}") for i in range(RING // GROUP)]
        gathered = sem("gathered")
        batch_used = sem("batch_used")
        onehot_ready = sem("onehot_ready")
        edge_ready = sem("edge_ready")
        first_copied = sem("first_copied")
        firstT_ready = sem("firstT_ready")
        firstT_copied = sem("firstT_copied")
        first_typed = sem("first_typed")
        first_hi = sem("first_hi")
        first_left = sem("first_left")
        first_mid = sem("first_mid")
        first_lo = sem("first_lo")
        first_written = [sem(f"first_written{i}") for i in range(2)]
        agg_ready = sem("agg_ready")
        sum_ready = sem("sum_ready")
        aggT_ready = sem("aggT_ready")
        aggT_copied = sem("aggT_copied")
        hT_cur_ready = sem("hT_cur_ready")
        gates_ready = sem("gates_ready")
        sig_ready = sem("sig_ready")
        cand_ready = sem("cand_ready")
        tanh_ready = sem("tanh_ready")
        row_ready = sem("row_ready")
        rowT_ready = sem("rowT_ready")
        rowT_copied = sem("rowT_copied")
        typed_ready = sem("typed_ready")
        source_ready = sem("source_ready")
        hi_ready = sem("hi_ready")
        rest_ready = sem("rest_ready")
        mid_ready = sem("mid_ready")
        lo_ready = sem("lo_ready")
        table_written = sem("table_written")
        u_ready = sem("u_ready")
        u_copied = sem("u_copied")
        v_ready = sem("v_ready")
        v_copied = sem("v_copied")
        var_ready = sem("var_ready")
        std_ready = sem("std_ready")
        o_ready = sem("o_ready")
        o_biased = sem("o_biased")
        relu_done = sem("relu_done")
        deg_ready = sem("deg_ready")
        deg_root = sem("deg_root")
        bn_mean = sem("bn_mean")
        bn_centred = sem("bn_centred")
        bn_squared = sem("bn_squared")
        bn_var = sem("bn_var")
        bn_var_copied = sem("bn_var_copied")
        bn_std = sem("bn_std")
        bn_scale = sem("bn_scale")
        ch_scaled = sem("ch_scaled")
        ch_centred = sem("ch_centred")
        ch_squared = sem("ch_squared")
        ch_var = sem("ch_var")
        ch_std = sem("ch_std")
        ch_done = sem("ch_done")
        ch_hi = sem("ch_hi")
        ch_rest = sem("ch_rest")
        ch_mid = sem("ch_mid")
        ch_lo = sem("ch_lo")
        sage_written = [sem(f"sage_written{i}") for i in range(4)]
        x_cur_ready = sem("x_cur_ready")
        xT_ready = sem("xT_ready")
        xT_copied = sem("xT_copied")
        out_ready = sem("out_ready")
        out_written = sem("out_written")

        block = ctx.enter_context(nc.Block())

        EDGE_ROWS = E // TP
        EDGE_REST = E - EDGE_ROWS * TP
        LOADS = 4 * 3 + 25
        ALL_LOADED = 16 * LOADS

        @block.sync
        def _(sp):
            sp.wait_ge(pads_set, 2)
            def load_x(to, done):
                sp.dma_start(to[:, 0:NT - 1, :],
                             x[0:(NT - 1) * P, :].rearrange("(d p) f -> p d f", p=P)).then_inc(done, 16)
                sp.dma_start(to[0:LAST, NT - 1, :], x[(NT - 1) * P:N, :]).then_inc(done, 16)

            load_x(x_all, x_loaded)
            for a, t in ((0, src), (1, dst), (2, edge_type), (3, edge_weight)):
                to = raw[:, 3, :] if a == 3 else raw_i[:, a, :]
                for r0, r1 in ((0, 112), (112, EDGE_ROWS)):
                    sp.dma_start(to[r0:r1, :], t[r0 * TP:r1 * TP].rearrange("(p n) -> p n", n=TP)
                                 ).then_inc(loaded, 16)
                sp.dma_start(to[EDGE_ROWS:EDGE_ROWS + 1, 0:EDGE_REST],
                             t[EDGE_ROWS * TP:E].rearrange("(p n) -> p n", p=1)).then_inc(loaded, 16)
            load_x(h_all, state_loaded)

            sp.wait_ge(edges_copied, TR)
            for p in range(PASSES):
                idx = typed_idx if p < STEPS else src_idx

                if p == 0:
                    def store_first(b, q):
                        sp.wait_ge(first_lo, b + 1)
                        sp.dma_start(typed[0].ap().rearrange("(n k) f -> n (k f)", k=K)[ds(b * PB * P, PB * P), :]
                                     .rearrange("(t p) f -> p t f", p=P),
                                     first_stage[:, q, :].rearrange("p (t f) -> p t f", t=PB)
                                     ).then_inc(first_written[q], 16)

                    with sp.Fori(0, NPB // 2) as i:
                        store_first(i * 2, 0)
                        store_first(i * 2 + 1, 1)
                    store_first(NPB - 1, 0)

                def stage_block(b, half):
                    sp.dma_start(idx_stage[:, half, :], idx[:, ds(b * BLOCK, BLOCK)]
                                 ).then_inc(idx_staged[half], 16)

                def relay(i, g):
                    sp.wait_ge(group_landed[g], (i + 1 + ROUNDS * p) * 16 * GROUP)
                    sp.sem_inc(gathered, GROUP // B)

                stage_block(0, 0)
                stage_block(1, 1)
                half = RING // GROUP // 2
                with sp.Fori(0, ROUNDS - 1) as i:
                    for g in range(half):
                        relay(i, g)
                    stage_block(i * 2 + 2, 0)
                    for g in range(half, 2 * half):
                        relay(i, g)
                    stage_block(i * 2 + 3, 1)
                for g in range(2 * half):
                    relay(ROUNDS - 1, g)
                if p == GCN:
                    for c in range(NCH):
                        sp.wait_ge(ch_lo, c + 1)
                        sp.dma_start(sage_table.ap()[c * CH * P:(c + 1) * CH * P, :]
                                     .rearrange("(d p) f -> p d f", p=P), ring_stage[:, c % 4]
                                     ).then_inc(sage_written[c % 4], 16)

        @block.gpsimd
        def _(pool):
            nc.gpsimd.memset(raw_i[:, 0, :], 0)
            nc.gpsimd.memset(raw_i[:, 1, :], NO_NODE)
            nc.gpsimd.memset(raw_i[:, 2, :], 0)
            nc.gpsimd.memset(raw[:, 3, :], 0.0).then_inc(pads_set, 1)
            nc.gpsimd.memset(h_all[:, NT - 1, :], 0.0)
            nc.gpsimd.memset(x_all[:, NT - 1, :], 0.0).then_inc(pads_set, 1)
            nc.gpsimd.iota(iota_row[:, :], pattern=[[1, P]], base=0, channel_multiplier=0,
                           allow_small_or_imprecise_dtypes=True)
            nc.gpsimd.iota(iota_col[:, :], pattern=[[0, 1]], base=0, channel_multiplier=1,
                           allow_small_or_imprecise_dtypes=True)
            nc.gpsimd.iota(bound_col[:, :], pattern=[[0, 1]], base=P, channel_multiplier=P,
                           allow_small_or_imprecise_dtypes=True)
            nc.gpsimd.memset(zeros[:, :], 0.0)
            nc.gpsimd.memset(zero_row[:, :], 0.0)
            nc.gpsimd.memset(ones_bf[:, :], 1.0)
            nc.gpsimd.memset(ones_row[:, :], 1.0)
            nc.gpsimd.memset(ones_mean[:, :], 1.0 / N)
            nc.gpsimd.memset(eps_col[:, :], EPS)
            nc.gpsimd.memset(first_open[:, 0:1], 0)
            nc.gpsimd.iota(first_ids[:, :, :], pattern=[[1, P], [0, B]], base=-P, channel_multiplier=0)
            nc.gpsimd.memset(first_x[:, :, :], 0.0)
            nc.gpsimd.memset(gate_in_w[:, 3 * H:4 * H], 0.0)
            nc.gpsimd.memset(gate_h_w[:, 2 * H:3 * H], 0.0)
            nc.gpsimd.memset(agg_sum[:, :], 0.0)
            nc.gpsimd.memset(row_new[:, :], 0.0)
            pool.drain()
            for t in (aggT, hT_cur, hT_new):
                nc.gpsimd.memset(t[H:H + 1, :], 1.0)
            nc.gpsimd.memset(firstT[H:H + 1, :, :], 1.0)
            pool.drain().then_inc(consts_made, 1)

            pool.wait_ge(x_loaded, 32)

            def copy_first(b, q):
                nc.gpsimd.tensor_copy(first_x[:, q, 0:PB * H],
                                      x_all[:, ds(b * PB, PB), :].rearrange("p t f -> p (t f)")
                                      ).then_inc(first_copied, 1)

            copy_first(0, 0)
            copy_first(1, 1)
            with pool.Fori(1, NPB // 2) as i:
                for q in range(2):
                    pool.wait_ge(firstT_ready, i * 2 + q - 1)
                    pool.sem_inc(pool_go, 1)
                    copy_first(i * 2 + q, q)
            pool.wait_ge(firstT_ready, NPB - 2)
            copy_first(NPB - 1, 0)

            for p in range(PASSES):
                F3 = 3 * width(p)
                slots = RING * H // width(p)
                if p == 0:
                    for q in range(2):
                        pool.wait_ge(first_written[q], 16 * len(range(q, NPB, 2)))
                elif p < SAGE:
                    pool.wait_ge(table_written, 16 * NT * p)
                else:
                    for i in range(4):
                        pool.wait_ge(sage_written[i], 16 * len(range(i, NCH, 4)))
                pool.sem_inc(pool_go, 1)
                with pool.Fori(0, ROUNDS) as i:
                    for t in range(RING):
                        if t % BLOCK == 0:
                            pool.wait_ge(idx_staged[t // BLOCK], (i + 1 + ROUNDS * p) * 16)
                            pool.sem_inc(pool_go, 1)
                        if t % GROUP == 0:
                            pool.wait_ge(batch_used, i * (RING // B)
                                         + (FULL * p + CREDIT + (t + GROUP - slots) // B))
                            pool.sem_inc(pool_go, 1)
                        s = t % slots
                        pool.indirect_dma_start(
                            out=ring[:, s * F3:(s + 1) * F3], out_offset=None, in_=tables[p].ap(),
                            in_offset=bass.IndirectOffsetOnAxis(
                                ap=idx_stage[:, t // BLOCK, t % BLOCK:t % BLOCK + 1], axis=0)
                        ).then_inc(group_landed[t // GROUP], 16)

                if p == GCN:
                    pool.wait_ge(bn_scale, 1)
                    for c in range(NCH):
                        hc = h_all[:, c * CH:(c + 1) * CH, :]
                        nc.gpsimd.tensor_tensor(hc, hc, gamma_all[:, :].rearrange("p (o f) -> p o f", o=1)
                                                .to_broadcast([P, CH, H]), ALU.mult).then_inc(ch_scaled, 1)
                    for c in range(NCH):
                        st = ring_stage[:, c % 4]
                        pool.wait_ge(ch_mid, c + 1)
                        nc.gpsimd.tensor_tensor(
                            st[:, :, 2 * H:3 * H],
                            squares.rearrange("p (d f) -> p d f", f=H)[:, c * CH:(c + 1) * CH, :],
                            st[:, :, H:2 * H], ALU.subtract).then_inc(ch_lo, 1)

        @block.tensor
        def _(pe):
            pe.wait_ge(loaded, ALL_LOADED)
            pe.wait_ge(dve_consts, 1)
            nc.tensor.transpose(ps_T[0:H, 0:P], raw_w[:, 0, :], ident[:, :])
            nc.tensor.transpose(ps_T[0:H, P:2 * P], raw_w[:, 1, :], ident[:, :])
            nc.tensor.transpose(ps_T[0:H, 2 * P:3 * P], raw_w[:, 2, :], ident[:, :])
            nc.tensor.transpose(ps_T[0:H, 3 * P:3 * P + H], raw_w[0:H, 3, :], ident[0:H, 0:H])
            nc.tensor.transpose(ps_gates[0:H, 0:P], raw_w[:, 4, :], ident[:, :])
            nc.tensor.transpose(ps_gates[0:H, P:P + H], raw_w[0:H, 5, :], ident[0:H, 0:H])
            nc.tensor.transpose(ps_gates[0:H, 2 * P:2 * P + H], raw_w[0:H, 6, :], ident[0:H, 0:H])
            nc.tensor.transpose(ps_gates[0:H, 3 * P:3 * P + H], raw_w[0:H, 7, :], ident[0:H, 0:H]
                                ).then_inc(w_turned, 1)
            pe.wait_ge(edges_linear, 1)
            turn = [ps_u, ps_v]
            for j in range(TR):
                if j >= 2:
                    pe.wait_ge(edges_copied, j - 1)
                for a, t in enumerate((src_lin, typed_lin, dst_lin, raw_w_e)):
                    last = nc.tensor.transpose(turn[j % 2][:, a * P:(a + 1) * P], t[:, j * P:(j + 1) * P],
                                               ident[:, :])
                last.then_inc(edges_turned, 1)
            pe.wait_ge(edges_copied, TR)
            nc.tensor.matmul(ps_agg[0:NT, 0:TP // B], pick_last[:, :],
                             dst_f[:, :].rearrange("e (g b) -> e b g", b=B)[:, B - 1, :],
                             start=True, stop=True).then_inc(last_dst, 1)
            pe.wait_ge(open_counted, 1)
            nc.tensor.matmul(ps_count[0:1, 0:NT], open_col[0:NT, :], ident[0:NT, 0:NT],
                             start=True, stop=True).then_inc(open_turned, 1)
            pe.wait_ge(w_copied, 1)

            def typed_rows(p, d):
                pe.wait_ge(row_ready, NT * p + 1 + d)
                nc.tensor.transpose(ps_T2[:, 0:P], row_new[:, :], ident[:, :]).then_inc(rowT_ready, 1)
                pe.wait_ge(rowT_copied, NT * p + 1 + d)
                nc.tensor.matmul(ps_typed[:, 0:K * H], hT_new[:, :], typed_w[:, :],
                                 start=True, stop=True).then_inc(typed_ready, 1)

            first_T, first_M = (ps_T, ps_T2), (ps_typed, ps_gates)

            def turn_first(b, q, warm):
                pe.wait_ge(first_copied, b + 1)
                if warm:
                    pe.wait_ge(firstT_copied, b - 1)
                for t in range(PB):
                    last = nc.tensor.transpose(first_T[q][:, t * P:(t + 1) * P],
                                               first_x[:, q, t * H:t * H + P], ident[:, :])
                last.then_inc(firstT_ready, 1)

            def type_first(b, q, warm):
                pe.wait_ge(firstT_copied, b + 1)
                if warm:
                    pe.wait_ge(first_left, b - 1)
                for t in range(PB):
                    last = nc.tensor.matmul(first_M[q][:, t * K * H:(t + 1) * K * H], firstT[:, q, t * P:(t + 1) * P],
                                            typed_w[:, :], start=True, stop=True)
                last.then_inc(first_typed, 1)

            turn_first(0, 0, False)
            turn_first(1, 1, False)
            type_first(0, 0, False)
            turn_first(2, 0, True)
            type_first(1, 1, False)
            with pe.Fori(1, NPB // 2) as i:
                turn_first(i * 2 + 1, 1, True)
                type_first(i * 2, 0, True)
                turn_first(i * 2 + 2, 0, True)
                type_first(i * 2 + 1, 1, True)
            type_first(NPB - 1, 0, True)
            pe.wait_ge(open_ready, 1)

            for p in range(PASSES):
                F3 = 3 * width(p)
                slots = RING * H // width(p)
                parts = 3 if p == SAGE else 1

                oh_slots = OHS_W if p == SAGE else OHS

                def batch_product(onehots, g, last):
                    row0 = pe.snap((g % (slots // B)) * (B * F3))
                    for k in range(parts * B):
                        end = last and k == parts * B - 1
                        oh = onehots(k // B).rearrange("p (n b) -> p b n", b=B)[:, k % B, :]
                        if p == 0:
                            nc.tensor.matmul(ps_count[:, 0:1], oh, ones_bf[:, :], start=False, stop=end)
                        ins = nc.tensor.matmul(ps_agg[:, 0:F3], oh, ring[:, ds(row0 + (k % B) * F3, F3)],
                                               start=False, stop=end)
                    return ins

                def node_tile(d):
                    lo = pe.value_load(first_open[0:1, ds(d, 1)], min_val=0, max_val=FULL)
                    hi = pe.value_load(first_open[0:1, ds(d + 1, 1)], min_val=0, max_val=FULL)
                    nc.tensor.matmul(ps_agg[:, 0:F3], zeros[:, 0:P], zeros[:, 0:F3], start=True, stop=False)
                    if p == 0:
                        nc.tensor.matmul(ps_count[:, 0:1], zeros[:, 0:P], zeros[:, 0:1], start=True, stop=False)
                    with pe.If(lo < hi):
                        with pe.Fori(lo, hi) as g:
                            pe.wait_ge(onehot_ready, g + (1 + FULL * p))
                            pe.wait_ge(gathered, g + (1 + TP // B * p))
                            slot = pe.snap((g % oh_slots) * (parts * B * P))
                            batch_product(lambda a: onehot[:, ds(slot + a * (B * P), B * P)], g, False
                                          ).then_inc(batch_used, 1)
                    pe.wait_ge(edge_ready, d + (1 + (NT + 1) * p))
                    pe.wait_ge(gathered, hi + (1 + TP // B * p))
                    batch_product(lambda a: onehot_edge[:, a * B * P:(a + 1) * B * P], hi, True).then_inc(agg_ready, 1)
                    here = NT * p + 1
                    if p == SAGE:
                        pe.wait_ge(x_cur_ready, d + 1)
                        nc.tensor.transpose(ps_T2[:, 0:P], row_new[:, :], ident[:, :]).then_inc(xT_ready, 1)
                    pe.wait_ge(sum_ready, here + d)
                    nc.tensor.transpose(ps_T[:, 0:P], agg_sum[:, :], ident[:, :]).then_inc(aggT_ready, 1)
                    if p < STEPS:
                        pe.wait_ge(hT_cur_ready, here + d)
                        nc.tensor.matmul(ps_gates[:, 0:4 * H], hT_cur[:, :], gate_h_w[:, :],
                                         start=True, stop=False)
                        pe.wait_ge(aggT_copied, here + d)
                        nc.tensor.matmul(ps_gates[:, 0:4 * H], aggT[:, :], gate_in_w[:, :],
                                         start=False, stop=True).then_inc(gates_ready, 1)
                        if p < STEPS - 1:
                            typed_rows(p, d)
                    elif p in (GIN1, GIN2):
                        base = NT * (p - GIN1) + 1
                        pe.wait_ge(aggT_copied, here + d)
                        if p == GIN1:
                            nc.tensor.matmul(ps_u[:, 0:P], w1a[:, :], aggT[0:H, :],
                                             start=True, stop=True).then_inc(u_ready, 1)
                        else:
                            nc.tensor.matmul(ps_u[:, 0:P], w2a[:, :], aggT_wide[:, :],
                                             start=True, stop=True).then_inc(u_ready, 1)
                        pe.wait_ge(u_copied, base + d)
                        O = HID if p == GIN1 else H
                        nc.tensor.matmul(ps_v[:, 0:O], uT[:, :], (w1b if p == GIN1 else w2b)[:, :],
                                         start=True, stop=False)
                        nc.tensor.matmul(ps_v[:, 0:O], ones_row[:, :], b1b_row if p == GIN1 else b2b_row,
                                         start=False, stop=True).then_inc(v_ready, 1)
                    elif p == GCN:
                        pe.wait_ge(aggT_copied, here + d)
                        nc.tensor.matmul(ps_u[:, 0:H], aggT[0:H, :], gcn_w[:, :],
                                         start=True, stop=True).then_inc(o_ready, 1)
                        pe.wait_ge(relu_done, d + 1)
                        last_tile = isinstance(d, int)
                        if not last_tile:
                            nc.tensor.matmul(ps_count[:, 0:H], ones_mean[:, :],
                                             h_all[:, ds(d, 1), :].rearrange("p o f -> p (o f)"),
                                             start=False, stop=False)
                        else:
                            nc.tensor.matmul(ps_count[:, 0:H], mean_last[:, :], h_all[:, d, :],
                                             start=False, stop=True).then_inc(bn_mean, 1)
                    else:
                        pe.wait_ge(xT_copied, d + 1)
                        nc.tensor.matmul(ps_v[:, 0:H], hT_new[0:H, :], self_wT[:, :], start=True, stop=False)
                        nc.tensor.matmul(ps_v[:, 0:H], ones_row[:, :], b_self_row, start=False, stop=False)
                        nc.tensor.matmul(ps_v[:, 0:H], ones_row[:, :], b_neigh_row, start=False, stop=True)
                        pe.wait_ge(aggT_copied, here + d)
                        nc.tensor.matmul(ps_u[:, 0:H], aggT[0:H, :], neigh_wT[:, :],
                                         start=True, stop=True).then_inc(o_ready, 1)

                if p == GCN:
                    nc.tensor.matmul(ps_count[:, 0:H], ones_mean[:, :], zero_row[:, :], start=True, stop=False)
                if p < GCN:
                    with pe.Fori(0, NT) as d:
                        node_tile(d)
                else:
                    with pe.Fori(0, NT - 1) as d:
                        node_tile(d)
                    node_tile(NT - 1)

                if p == GCN:
                    cols, part = CH * H, CH * H // 2
                    for c in range(NCH):
                        pe.wait_ge(bn_squared, c + 1)
                        for k in range(2):
                            last = nc.tensor.matmul(ps_u[:, 0:part], ones_mean[:, :],
                                                    squares[:, c * cols + k * part:c * cols + (k + 1) * part],
                                                    start=c + k == 0, stop=c == NCH - 1 and k == 1)
                    last.then_inc(bn_var, 1)

        @block.scalar
        def _(act):
            pieces = [
                (raw_w[:, 0:2, :], g_W.rearrange("(c k) h d -> (k h) c d", c=2)),
                (raw_w[:, 2, :], g_w_ih[0:P, :]), (raw_w[0:H, 3, :], g_w_ih[P:3 * H, :]),
                (raw_w[:, 4, :], g_w_hh[0:P, :]), (raw_w[0:H, 5, :], g_w_hh[P:3 * H, :]),
                (raw_w[0:H, 6, :], W_self), (raw_w[0:H, 7, :], W_neigh),
                (typed_w[H:H + 1, :], g_b.rearrange("(o k) h -> o (k h)", o=1)),
                (gate_in_w[H:H + 1, 0:3 * H], g_b_ih.rearrange("(o n) -> o n", o=1)),
                (gate_h_w[H:H + 1, 0:2 * H], g_b_hh[0:2 * H].rearrange("(o n) -> o n", o=1)),
                (gate_h_w[H:H + 1, 3 * H:4 * H], g_b_hh[2 * H:3 * H].rearrange("(o n) -> o n", o=1)),
                (w1a[:, :], W1a), (w1b[:, :], W1b), (w2a[:, :], W2a), (w2b[:, :], W2b),
                (b1a_col[:, :], b1a.rearrange("(n o) -> n o", o=1)),
                (b2a_col[:, :], b2a.rearrange("(n o) -> n o", o=1)),
                (rows[0:1, 0:HID], b1b.rearrange("(o n) -> o n", o=1)),
                (rows[0:1, HID:HID + H], b2b.rearrange("(o n) -> o n", o=1)),
                (rows[0:1, HID + H:HID + 2 * H], b_self.rearrange("(o n) -> o n", o=1)),
                (rows[0:1, HID + 2 * H:HID + 3 * H], b_neigh.rearrange("(o n) -> o n", o=1)),
                (gcn_w[:, :], gcn_W),
            ]
            act.wait_ge(consts_made, 1)
            for to, frm in pieces:
                act.dma_start(to, frm).then_inc(loaded, 16)
            for to, frm in ((gcn_b_all, gcn_b), (gamma_all, gamma), (beta_all, beta)):
                act.dma_start(to[:, :], frm.rearrange("(o n) -> o n", o=1).to_broadcast([P, H])
                              ).then_inc(loaded, 16)
            assert len(pieces) + 3 + 12 == LOADS, len(pieces)

            def split_and_store(p, d, source, groups, W, table_rows):
                at = NT * p + d
                hi, mid = stage_parts(groups, W)[0:2]
                act.activation(hi, source, ACT.Copy).then_inc(hi_ready, 1)
                act.wait_ge(rest_ready, at + 1)
                act.activation(mid, rest[:, 0:groups * W].rearrange("p (k w) -> p k w", k=groups), ACT.Copy
                               ).then_inc(mid_ready, 1)
                act.wait_ge(lo_ready, at + 1)
                act.dma_start(table_rows, stage_flat[:, 0:3 * W * groups]).then_inc(table_written, 16)
                act.wait_ge(table_written, at * 16 + 16)

            stage_flat = stage[:, :, :].rearrange("p k n -> p (k n)")

            def stage_parts(groups, W):
                v = stage_flat[:, 0:3 * W * groups].rearrange("p (k a w) -> p k a w", k=groups, a=3)
                return [v[:, :, a, :] for a in range(3)]

            def typed_rows(p, d):
                at = NT * p + 1
                act.wait_ge(rowT_ready, at + d)
                act.activation(hT_new[0:H, :], ps_T2[0:H, 0:P], ACT.Copy).then_inc(rowT_copied, 1)
                act.activation(featT[:, ds(d * P, P)], ps_T2[0:H, 0:P], ACT.Copy)
                act.wait_ge(typed_ready, at + d)
                to = typed[(p + 1) % 2].ap().rearrange("(n k) f -> n (k f)", k=K)[ds(d * P, P), :]
                split_and_store(p, d, ps_typed[:, 0:K * H].rearrange("p (k w) -> p k w", k=K), K, H, to)

            first_T, first_M = (ps_T, ps_T2), (ps_typed, ps_gates)

            def first_part(t, a):
                return t.rearrange("p (k a w) -> p k a w", k=PB * K, a=3)[:, :, a, :]

            def copy_firstT(b, q, warm):
                act.wait_ge(firstT_ready, b + 1)
                if warm:
                    act.wait_ge(first_typed, b - 1)
                act.activation(firstT[0:H, q, :], first_T[q][0:H, 0:PB * P], ACT.Copy).then_inc(firstT_copied, 1)

            def hi_first(b, q, round_):
                act.wait_ge(first_typed, b + 1)
                if round_ is not None:
                    act.wait_ge(first_written[q], round_ * 16)
                act.activation(first_part(first_stage[:, q, :], 0),
                               first_M[q][:, :].rearrange("p (k w) -> p k w", w=H), ACT.Copy).then_inc(first_hi, 1)

            def mid_first(b, q):
                act.wait_ge(first_left, b + 1)
                act.activation(first_part(first_stage[:, q, :], 1),
                               first_rest[:, q, :].rearrange("p (k w) -> p k w", w=H), ACT.Copy
                               ).then_inc(first_mid, 1)

            copy_firstT(0, 0, False)
            copy_firstT(1, 1, False)
            hi_first(0, 0, None)
            hi_first(1, 1, None)
            mid_first(0, 0)
            copy_firstT(2, 0, True)
            with act.Fori(1, NPB // 2) as i:
                hi_first(i * 2, 0, i)
                mid_first(i * 2 - 1, 1)
                copy_firstT(i * 2 + 1, 1, True)
                hi_first(i * 2 + 1, 1, i)
                mid_first(i * 2, 0)
                copy_firstT(i * 2 + 2, 0, True)
            hi_first(NPB - 1, 0, NPB // 2)
            mid_first(NPB - 2, 1)
            mid_first(NPB - 1, 0)

            def layernorm_root(k, d):
                act.wait_ge(var_ready, NT * k + 1 + d)
                act.activation(std[:, 0:1], moments[:, 1:2], ACT.Sqrt, bias=eps_col[:, :]).then_inc(std_ready, 1)

            for p in range(PASSES):
                here = NT * p + 1
                if p == 1:
                    act.wait_ge(deg_ready, 1)
                    act.activation(deg_rsqrt[:, :], std[:, :], ACT.Sqrt).then_inc(deg_root, 1)

                def node_tile(d):
                    if p < STEPS:
                        act.activation(hT_cur[0:H, :], featT[:, ds(d * P, P)], ACT.Copy
                                       ).then_inc(hT_cur_ready, 1)
                    if p == SAGE:
                        act.wait_ge(xT_ready, d + 1)
                        act.activation(hT_new[0:H, :], ps_T2[0:H, 0:P], ACT.Copy).then_inc(xT_copied, 1)
                    act.wait_ge(aggT_ready, here + d)
                    if p == GIN2:
                        act.activation(aggT_wide[:, :], ps_T[:, 0:P], ACT.Copy).then_inc(aggT_copied, 1)
                    else:
                        act.activation(aggT[0:H, :], ps_T[0:H, 0:P], ACT.Copy).then_inc(aggT_copied, 1)
                    if p < STEPS:
                        act.wait_ge(gates_ready, here + d)
                        act.activation(gates[:, :], ps_gates[:, 0:2 * H], ACT.Tanh, scale=0.5
                                       ).then_inc(sig_ready, 1)
                        act.wait_ge(cand_ready, here + d)
                        act.activation(cand_act[:, :], cand[:, :], ACT.Tanh).then_inc(tanh_ready, 1)
                        if p < STEPS - 1:
                            typed_rows(p, d)
                        else:
                            layernorm_root(0, d)
                            act.wait_ge(source_ready, d + 1)
                            split_and_store(p, d, row_new[:, 0:H].rearrange("p (k w) -> p k w", k=1), 1, H,
                                            gin1_table.ap()[ds(d * P, P), :])
                    elif p in (GIN1, GIN2):
                        base = NT * (p - GIN1) + 1
                        act.wait_ge(u_ready, base + d)
                        act.activation(uT[:, :], ps_u[:, 0:P], ACT.Relu,
                                       bias=(b1a_col if p == GIN1 else b2a_col)[:, :]).then_inc(u_copied, 1)
                        act.wait_ge(v_ready, base + d)
                        if p == GIN1:
                            act.activation(row_new[:, :], ps_v[:, 0:HID], ACT.Relu).then_inc(v_copied, 1)
                            act.drain()
                            split_and_store(p, d, row_new[:, :].rearrange("p (k w) -> p k w", k=1), 1, HID,
                                            gin2_table.ap()[ds(d * P, P), :])
                        else:
                            act.activation(v_row[:, :], ps_v[:, 0:H], ACT.Relu).then_inc(v_copied, 1)
                            layernorm_root(1, d)
                            act.wait_ge(source_ready, NT + 1 + d)
                            split_and_store(p, d, row_new[:, 0:H].rearrange("p (k w) -> p k w", k=1), 1, H,
                                            gcn_table.ap()[ds(d * P, P), :])
                    elif p == GCN:
                        act.wait_ge(o_biased, d + 1)
                        act.activation(h_all[:, ds(d, 1), :].rearrange("p o f -> p (o f)"), o_row[:, :], ACT.Relu
                                       ).then_inc(relu_done, 1)
                    else:
                        layernorm_root(2, d)
                        act.wait_ge(out_ready, d + 1)
                        if isinstance(d, int):
                            act.dma_start(out[d * P:N, :], out_row[0:LAST, :]).then_inc(out_written, 16)
                        else:
                            act.dma_start(out[ds(d * P, P), :], out_row[:, :]).then_inc(out_written, 16)
                        act.wait_ge(out_written, d * 16 + 16)

                if p < GCN:
                    with act.Fori(0, NT) as d:
                        node_tile(d)
                else:
                    with act.Fori(0, NT - 1) as d:
                        node_tile(d)
                    node_tile(NT - 1)
                if p == SAGE:
                    act.wait_ge(out_written, 16 * NT)

                if p == GCN:
                    def chunk(c):
                        sq = squares.rearrange("p (d f) -> p d f", f=H)[:, c * CH:(c + 1) * CH, :]
                        return (h_all[:, c * CH:(c + 1) * CH, :], sq, x_all[:, c * CH:(c + 1) * CH, :],
                                ring_stage[:, c % 4])

                    for c in range(NCH):
                        hc, sq, xc, st = chunk(c)
                        act.wait_ge(bn_centred, c + 1)
                        act.activation(sq, hc, ACT.Square).then_inc(bn_squared, 1)
                    act.wait_ge(bn_var_copied, 1)
                    act.activation(var_all[:, :], var_all[:, :], ACT.Sqrt, bias=eps_col[:, :]).then_inc(bn_std, 1)

                    def square(c):
                        hc, sq, xc, st = chunk(c)
                        act.wait_ge(ch_centred, c + 1)
                        act.activation(sq, hc, ACT.Square).then_inc(ch_squared, 1)

                    def root(c):
                        act.wait_ge(ch_var, c + 1)
                        act.activation(std[:, c * CH:(c + 1) * CH], ln_rstd[:, c * CH:(c + 1) * CH], ACT.Sqrt,
                                       bias=eps_col[:, :], scale=1.0 / H).then_inc(ch_std, 1)

                    def high(c):
                        hc, sq, xc, st = chunk(c)
                        act.wait_ge(ch_done, c + 1)
                        if c >= 4:
                            act.wait_ge(sage_written[c % 4], 16)
                        act.activation(st[:, :, 0:H], xc, ACT.Copy).then_inc(ch_hi, 1)

                    def middle(c):
                        hc, sq, xc, st = chunk(c)
                        act.wait_ge(ch_rest, c + 1)
                        act.activation(st[:, :, H:2 * H], sq, ACT.Copy).then_inc(ch_mid, 1)

                    for c in range(NCH + 2):
                        if c < NCH:
                            square(c)
                        if 1 <= c <= NCH:
                            root(c - 1)
                            high(c - 1)
                        if c >= 2:
                            middle(c - 2)

        @block.vector
        def _(dve):
            dve.sem_inc(batch_used, CREDIT)
            dve.wait_ge(consts_made, 1)
            v = nc.vector
            v.tensor_scalar(ident[:, :], iota_row[:, :], iota_col[:, :], None, ALU.is_equal)
            v.tensor_scalar(pick_last[:, :], iota_col[:, :].to_broadcast([P, NT]), float(P - 1), None, ALU.is_equal)
            v.tensor_scalar(mask_last[:, :], iota_col[:, :], float(LAST), None, ALU.is_lt)
            dve.drain().then_inc(dve_consts, 1)
            v.tensor_scalar(mean_last[:, :], ones_mean[:, :], mask_last[:, :], None, ALU.mult)
            dve.wait_ge(loaded, ALL_LOADED)
            v.scalar_tensor_tensor(out=typed_lin, in0=raw_src, scalar=float(K), in1=raw_type, op0=ALU.mult, op1=ALU.add)
            v.tensor_copy(src_lin, raw_src)
            v.tensor_copy(dst_lin, raw_dst).then_inc(edges_linear, 1)
            dve.wait_ge(w_turned, 1)
            v.tensor_copy(typed_w[0:H, :], ps_T[0:H, 0:2 * P])
            v.tensor_copy(gate_in_w[0:H, 0:3 * H], ps_T[0:H, 2 * P:2 * P + 3 * H])
            v.tensor_copy(gate_h_w[0:H, 0:2 * H], ps_gates[0:H, 0:2 * H])
            v.tensor_copy(gate_h_w[0:H, 3 * H:4 * H], ps_gates[0:H, 2 * H:3 * H])
            v.tensor_copy(self_wT[:, :], ps_gates[0:H, 2 * P:2 * P + H])
            v.tensor_copy(neigh_wT[:, :], ps_gates[0:H, 3 * P:3 * P + H]).then_inc(w_copied, 1)
            turn = [ps_u, ps_v]
            for j in range(TR):
                dve.wait_ge(edges_turned, j + 1)
                for a, to in enumerate((src_idx, typed_idx, dst_id, dst_f, w_f)):
                    last = v.tensor_copy(to[:, :].rearrange("e (p j) -> e j p", j=TR)[:, j, :],
                                         turn[j % 2][:, (0, 1, 2, 2, 3)[a] * P:((0, 1, 2, 2, 3)[a] + 1) * P])
                last.then_inc(edges_copied, 1)
            dve.wait_ge(last_dst, 1)
            v.tensor_scalar(below, ps_agg[0:NT, 0:TP // B], bound_col[0:NT, :], None, ALU.is_lt)
            dve.drain()
            v.reduce_sum(open_col[0:NT, :], below, axis=AX.X).then_inc(open_counted, 1)
            dve.wait_ge(open_turned, 1)
            v.tensor_copy(first_open[0:1, 1:NT + 1], ps_count[0:1, 0:NT])
            v.tensor_copy(first_open[0:1, NT + 1:NT + 2], ps_count[0:1, NT - 1:NT])
            dve.drain()
            v.tensor_scalar(ahead_end[:, :], first_open[:, 0:NT + 1], float(AHEAD), None, ALU.add)
            dve.drain()
            v.tensor_tensor(ahead_end[:, :], ahead_end[:, :], first_open[:, 1:NT + 2], ALU.min)
            dve.drain().then_inc(open_ready, 1)
            dve.wait_ge(open_ready, 1)

            def first_part(t, a):
                return t.rearrange("p (k a w) -> p k a w", k=PB * K, a=3)[:, :, a, :]

            def rest_first(b, q):
                dve.wait_ge(firstT_copied, b + 1)
                v.tensor_copy(featT[:, ds(b * PB * P, PB * P)], firstT[0:H, q, :])
                dve.wait_ge(first_hi, b + 1)
                v.tensor_tensor(first_rest[:, q, :].rearrange("p (k w) -> p k w", w=H),
                                (ps_typed, ps_gates)[q][:, :].rearrange("p (k w) -> p k w", w=H),
                                first_part(first_stage[:, q, :], 0), ALU.subtract).then_inc(first_left, 1)

            def lo_first(b, q):
                dve.wait_ge(first_mid, b + 1)
                v.tensor_tensor(first_part(first_stage[:, q, :], 2),
                                first_rest[:, q, :].rearrange("p (k w) -> p k w", w=H),
                                first_part(first_stage[:, q, :], 1), ALU.subtract).then_inc(first_lo, 1)

            rest_first(0, 0)
            with dve.Fori(0, NPB // 2) as i:
                rest_first(i * 2 + 1, 1)
                lo_first(i * 2, 0)
                rest_first(i * 2 + 2, 0)
                lo_first(i * 2 + 1, 1)
            lo_first(NPB - 1, 0)

            stage_flat = stage[:, :, :].rearrange("p k n -> p (k n)")

            def split(p, d, source, groups, W):
                at = NT * p + 1
                parts = stage_flat[:, 0:3 * W * groups].rearrange("p (k a w) -> p k a w", k=groups, a=3)
                r = rest[:, 0:groups * W].rearrange("p (k w) -> p k w", k=groups)
                dve.wait_ge(hi_ready, at + d)
                v.tensor_tensor(r, source, parts[:, :, 0, :], ALU.subtract).then_inc(rest_ready, 1)
                dve.wait_ge(mid_ready, at + d)
                v.tensor_tensor(parts[:, :, 2, :], r, parts[:, :, 1, :], ALU.subtract).then_inc(lo_ready, 1)

            def typed_rows(p, d):
                split(p, d, ps_typed[:, 0:K * H].rearrange("p (k w) -> p k w", k=K), K, H)

            def tile(t, d):
                return t[:, ds(d, 1), :].rearrange("p o f -> p (o f)")

            def layernorm(k, d, to):
                dve.drain()
                v.bn_stats(stats6[:, :], y_row[:, :])
                dve.drain()
                v.bn_aggr(moments[:, :], stats6[:, :]).then_inc(var_ready, 1)
                dve.wait_ge(std_ready, NT * k + 1 + d)
                v.reciprocal(rstd[:, :], std[:, 0:1])
                dve.drain()
                return v.tensor_scalar(to, y_row[:, :], moments[:, 0:1], rstd[:, :], ALU.subtract, ALU.mult)

            dve.wait_ge(x_loaded, 32)
            dve.wait_ge(state_loaded, 32)
            for p in range(PASSES):
                W = width(p)
                if p == 1:
                    v.tensor_scalar(inv_count[:, :], count[:, :], 1.0, None, ALU.max)
                    v.tensor_scalar(std[:, :], count[:, :], 1.0, 1.0, ALU.add, ALU.max).then_inc(deg_ready, 1)
                    dve.drain()
                    v.reciprocal(inv_count[:, :], inv_count[:, :])
                    dve.wait_ge(deg_root, 1)
                    v.reciprocal(deg_rsqrt[:, :], deg_rsqrt[:, :])
                if p == GCN:
                    dve.drain()
                    v.tensor_copy(w_parts[:, 0, :], w_f[:, :])
                    dve.drain()
                    v.tensor_tensor(w_left, w_f[:, :], w_parts[:, 0, :], ALU.subtract)
                    dve.drain()
                    v.tensor_copy(w_parts[:, 1, :], w_left)
                    dve.drain()
                    v.tensor_tensor(w_parts[:, 2, :], w_left, w_parts[:, 1, :], ALU.subtract)
                parts = 3 if p == SAGE else 1
                oh_slots = OHS_W if p == SAGE else OHS

                def make_onehots(to, g):
                    there = dst_id[:, ds(g * B, B)].rearrange("p (o b) -> p o b", o=1).to_broadcast([P, P, B])
                    if p < SAGE:
                        return v.tensor_tensor(to.rearrange("p (n b) -> p n b", b=B), node_ids[:, :, :], there,
                                               ALU.is_equal)
                    dve.drain()
                    v.tensor_tensor(matches[:, :, :], node_ids[:, :, :], there, ALU.is_equal)
                    dve.drain()
                    for a in range(3):
                        w = w_parts[:, a, :][:, ds(g * B, B)].rearrange("p (o b) -> p o b", o=1)
                        last = v.tensor_tensor(to[:, a * B * P:(a + 1) * B * P].rearrange("p (n b) -> p n b", b=B),
                                               matches[:, :, :], w.to_broadcast([P, P, B]), ALU.mult)
                    return last

                def full_onehots(lo, hi):
                    with dve.If(lo < hi):
                        with dve.Fori(lo, hi) as g:
                            if p == SAGE:
                                dve.wait_ge(batch_used, g + (FULL * p + CREDIT - oh_slots + 1))
                                dve.sem_inc(dve_go, 1)
                            else:
                                dve.wait_ge(batch_used, g + (FULL * p + CREDIT - oh_slots + 1))
                            slot = dve.snap((g % oh_slots) * (parts * B * P))
                            make_onehots(onehot[:, ds(slot, parts * B * P)], g).then_inc(onehot_ready, 1)

                def open_of(row, d):
                    return dve.value_load(row[0:1, ds(d, 1)], min_val=0, max_val=FULL)

                def onehots_ahead(d):
                    v.tensor_scalar(node_ids[:, :, :], node_ids[:, :, :], float(P), None, ALU.add)
                    dve.drain()
                    full_onehots(open_of(first_open, d), open_of(ahead_end, d))
                    make_onehots(onehot_edge[:, 0:parts * B * P], open_of(first_open, d + 1)
                                 ).then_inc(edge_ready, 1)

                v.tensor_copy(node_ids[:, :, :], first_ids[:, :, :])
                dve.drain()
                onehots_ahead(0)

                def node_tile(d):
                    full_onehots(open_of(ahead_end, d), open_of(first_open, d + 1))
                    if p == SAGE:
                        v.tensor_copy(row_new[:, 0:H], tile(x_all, d)).then_inc(x_cur_ready, 1)

                    here = NT * p + 1
                    dve.wait_ge(agg_ready, here + d)
                    if p == 0:
                        v.tensor_copy(count[:, ds(d, 1)], ps_count[:, 0:1])
                    v.tensor_copy(agg_sum[:, 0:W], ps_agg[:, 2 * W:3 * W])
                    dve.drain()
                    v.tensor_tensor(agg_sum[:, 0:W], ps_agg[:, W:2 * W], agg_sum[:, 0:W], ALU.add)
                    dve.drain()
                    last = v.tensor_tensor(agg_sum[:, 0:W], ps_agg[:, 0:W], agg_sum[:, 0:W], ALU.add)
                    if p in (GIN1, GIN2):
                        dve.drain()
                        last = v.tensor_tensor(agg_sum[:, 0:W], agg_sum[:, 0:W],
                                               tile(x_all if p == GIN1 else gin_h, d), ALU.add)
                    if p == GCN:
                        dve.drain()
                        last = v.scalar_tensor_tensor(out=agg_sum[:, 0:H], in0=tile(x_all, d),
                                                      scalar=deg_rsqrt[:, ds(d, 1)], in1=agg_sum[:, 0:H],
                                                      op0=ALU.mult, op1=ALU.add)
                    last.then_inc(sum_ready, 1)
                    if p == GCN:
                        dve.drain()
                        v.tensor_tensor(tile(x_all, d), tile(x_all, d), beta_all[:, :], ALU.add)
                    if p in (GIN1, GIN2, SAGE):
                        onehots_ahead(d + 1)

                    if p < STEPS:
                        dve.wait_ge(sig_ready, here + d)
                        v.scalar_tensor_tensor(out=cand[:, :], in0=gates[:, 0:H], scalar=1.0,
                                               in1=ps_gates[:, 3 * H:4 * H], op0=ALU.add, op1=ALU.mult)
                        dve.drain()
                        v.scalar_tensor_tensor(out=cand[:, :], in0=cand[:, :], scalar=0.5,
                                               in1=ps_gates[:, 2 * H:3 * H], op0=ALU.mult, op1=ALU.add
                                               ).then_inc(cand_ready, 1)
                        dve.wait_ge(tanh_ready, here + d)
                        v.tensor_tensor(diff[:, :], tile(h_all, d), cand_act[:, :], ALU.subtract)
                        dve.drain()
                        v.scalar_tensor_tensor(out=diff[:, :], in0=gates[:, H:2 * H], scalar=1.0, in1=diff[:, :],
                                               op0=ALU.add, op1=ALU.mult)
                        dve.drain()

                        def new_state(to):
                            return v.scalar_tensor_tensor(out=to, in0=diff[:, :], scalar=0.5, in1=cand_act[:, :],
                                                          op0=ALU.mult, op1=ALU.add)

                        if p < STEPS - 1:
                            new_state(row_new[:, 0:H]).then_inc(row_ready, 1)
                            dve.drain()
                            v.tensor_copy(tile(h_all, d), row_new[:, 0:H])
                            onehots_ahead(d + 1)
                            typed_rows(p, d)
                        else:
                            new_state(y_row[:, :])
                            dve.drain()
                            v.tensor_tensor(y_row[:, :], y_row[:, :], tile(x_all, d), ALU.add)
                            onehots_ahead(d + 1)
                            layernorm(0, d, row_new[:, 0:H]).then_inc(source_ready, 1)
                            dve.drain()
                            v.tensor_copy(tile(x_all, d), row_new[:, 0:H])
                            split(p, d, row_new[:, 0:H].rearrange("p (k w) -> p k w", k=1), 1, H)
                    elif p == GIN1:
                        dve.wait_ge(v_copied, d + 1)
                        v.tensor_copy(tile(gin_h, d), row_new[:, :])
                        split(p, d, row_new[:, :].rearrange("p (k w) -> p k w", k=1), 1, HID)
                    elif p == GIN2:
                        dve.wait_ge(v_copied, NT + 1 + d)
                        v.tensor_tensor(y_row[:, :], v_row[:, :], tile(x_all, d), ALU.add)
                        layernorm(1, d, o_row[:, :])
                        dve.drain()
                        v.tensor_copy(tile(x_all, d), o_row[:, :])
                        v.tensor_scalar(row_new[:, 0:H], o_row[:, :], deg_rsqrt[:, ds(d, 1)], None, ALU.mult
                                        ).then_inc(source_ready, 1)
                        dve.drain()
                        split(p, d, row_new[:, 0:H].rearrange("p (k w) -> p k w", k=1), 1, H)
                    elif p == GCN:
                        dve.wait_ge(o_ready, d + 1)
                        v.scalar_tensor_tensor(out=o_row[:, :], in0=ps_u[:, 0:H], scalar=deg_rsqrt[:, ds(d, 1)],
                                               in1=gcn_b_all[:, :], op0=ALU.mult, op1=ALU.add
                                               ).then_inc(o_biased, 1)
                        onehots_ahead(d + 1)
                        dve.wait_ge(relu_done, d + 1)
                    else:
                        dve.wait_ge(o_ready, NT + 1 + d)
                        v.tensor_copy(o_row[:, :], ps_v[:, 0:H])
                        dve.drain()
                        v.scalar_tensor_tensor(out=y_row[:, :], in0=ps_u[:, 0:H], scalar=inv_count[:, ds(d, 1)],
                                               in1=o_row[:, :], op0=ALU.mult, op1=ALU.add)
                        dve.drain()
                        v.tensor_tensor(y_row[:, :], y_row[:, :], tile(x_all, d), ALU.add)
                        layernorm(2, d, out_row[:, :]).then_inc(out_ready, 1)

                if p < GCN:
                    with dve.Fori(0, NT) as d:
                        node_tile(d)
                else:
                    with dve.Fori(0, NT - 1) as d:
                        node_tile(d)
                    node_tile(NT - 1)

                if p == GCN:
                    def over(t, n):
                        return t[:, :].rearrange("p (o f) -> p o f", o=1).to_broadcast([P, n, H])

                    def chunk(c):
                        sq = squares.rearrange("p (d f) -> p d f", f=H)[:, c * CH:(c + 1) * CH, :]
                        return (h_all[:, c * CH:(c + 1) * CH, :], sq, x_all[:, c * CH:(c + 1) * CH, :],
                                ring_stage[:, c % 4])

                    def per_node(t, c):
                        return t[:, c * CH:(c + 1) * CH].rearrange("p (d o) -> p d o", o=1).to_broadcast([P, CH, H])

                    dve.wait_ge(bn_mean, 1)
                    v.tensor_copy(mean_all[:, :], ps_count[:, 0:H])
                    dve.drain()
                    for c in range(NCH):
                        hc, sq, xc, st = chunk(c)
                        last = v.tensor_tensor(hc, hc, over(mean_all, CH), ALU.subtract)
                        if c == NCH - 1:
                            dve.drain()
                            last = v.tensor_scalar(h_all[:, NT - 1, :], h_all[:, NT - 1, :], mask_last[:, :], None,
                                                   ALU.mult)
                        last.then_inc(bn_centred, 1)
                    dve.wait_ge(bn_var, 1)
                    v.tensor_reduce(out=var_all[:, :], in_=ps_u[:, 0:CH * H // 2].rearrange("p (g c) -> p c g", c=H),
                                    axis=AX.X, op=ALU.add).then_inc(bn_var_copied, 1)
                    dve.wait_ge(bn_std, 1)
                    v.reciprocal(var_all[:, :], var_all[:, :])
                    dve.drain()
                    v.tensor_tensor(gamma_all[:, :], gamma_all[:, :], var_all[:, :], ALU.mult
                                    ).then_inc(bn_scale, 1)

                    def centre(c):
                        hc, sq, xc, st = chunk(c)
                        dve.drain()
                        dve.wait_ge(ch_scaled, c + 1)
                        v.tensor_tensor(hc, hc, xc, ALU.add)
                        dve.drain()
                        v.reduce_sum(ln_sum[:, c * CH:(c + 1) * CH], hc, axis=AX.X)
                        dve.drain()
                        v.tensor_scalar(ln_sum[:, c * CH:(c + 1) * CH], ln_sum[:, c * CH:(c + 1) * CH], 1.0 / H, None,
                                        ALU.mult)
                        dve.drain()
                        v.tensor_tensor(hc, hc, per_node(ln_sum, c), ALU.subtract).then_inc(ch_centred, 1)

                    def scale(c):
                        hc, sq, xc, st = chunk(c)
                        dve.wait_ge(ch_squared, c + 1)
                        v.reduce_sum(ln_rstd[:, c * CH:(c + 1) * CH], sq, axis=AX.X).then_inc(ch_var, 1)
                        dve.wait_ge(ch_std, c + 1)
                        v.reciprocal(ln_rstd[:, c * CH:(c + 1) * CH], std[:, c * CH:(c + 1) * CH])
                        dve.drain()
                        v.tensor_tensor(xc, hc, per_node(ln_rstd, c), ALU.mult).then_inc(ch_done, 1)

                    def leave(c):
                        hc, sq, xc, st = chunk(c)
                        dve.wait_ge(ch_hi, c + 1)
                        v.tensor_tensor(sq, xc, st[:, :, 0:H], ALU.subtract).then_inc(ch_rest, 1)

                    for c in range(NCH + 2):
                        if c < NCH:
                            centre(c)
                        if 1 <= c <= NCH:
                            scale(c - 1)
                        if c >= 2:
                            leave(c - 2)


_INS = ['x', 'src', 'dst', 'edge_type_4', 'edge_weight', 'L0_gnn_W', 'L0_gnn_b', 'L0_gnn_w_ih', 'L0_gnn_w_hh',
        'L0_gnn_b_ih', 'L0_gnn_b_hh', 'L1_gnn_W1a', 'L1_gnn_b1a', 'L1_gnn_W1b', 'L1_gnn_b1b', 'L1_gnn_W2a',
        'L1_gnn_b2a', 'L1_gnn_W2b', 'L1_gnn_b2b', 'L2_gnn_W', 'L2_gnn_b', 'L2_gnn_gamma', 'L2_gnn_beta',
        'L3_gnn_W_self', 'L3_gnn_b_self', 'L3_gnn_W_neigh', 'L3_gnn_b_neigh']


def kernel(**inputs):
    import numpy as _np
    import concourse.bacc as _bacc
    from concourse import mybir as _mybir
    from concourse.bass_utils import run_bass_kernel_spmd as _run

    nc = _bacc.Bacc("TRN2", target_bir_lowering=False, num_devices=1)
    arrays, args = {}, []
    for name in _INS:
        a = _np.ascontiguousarray(inputs[name])
        arrays[f"in_{name}"] = a
        args.append(nc.dram_tensor(f"in_{name}", a.shape, _mybir.dt.from_np(a.dtype), kind="ExternalInput").ap())
    out = nc.dram_tensor("out_0", (N, H), _mybir.dt.float32, kind="ExternalOutput").ap()
    build(nc, *args, out)
    r = _run(nc, [arrays], core_ids=[0])
    return r.results[0]["out_0"]
```

```python
import concourse.bass as bass
from concourse import mybir
from contextlib import ExitStack

N = 12500
H = 64
E = 212500
K = 4
HID = 128
P = 128
NT = -(-N // P)
NP = NT * P
LAST = N - (NT - 1) * P
RING = 64
GROUP = 8
BLOCK = 32
TP = -(-E // (P * RING)) * RING
B = 4
FULL = E // (P * B)
TR = TP // P
ROUNDS = TP // RING
OHS = 16
OHS_W = 8
CREDIT = 32
STORED = 16
AHEAD = OHS_W
PB = 2
NPB = NT // PB
FS = 4
EDGES_AT = 4
STEPS = 4
GIN1, GIN2, GCN, SAGE = 4, 5, 6, 7
PASSES = 8
EPS = 1e-5
CH = 14
NCH = NT // CH
NO_NODE = 20000


def build(nc, x, src, dst, edge_type, edge_weight, g_W, g_b, g_w_ih, g_w_hh, g_b_ih, g_b_hh,
          W1a, b1a, W1b, b1b, W2a, b2a, W2b, b2b, gcn_W, gcn_b, gamma, beta,
          W_self, b_self, W_neigh, b_neigh, out):
    fp32, bf16, i32, i16 = mybir.dt.float32, mybir.dt.bfloat16, mybir.dt.int32, mybir.dt.int16
    ALU, ACT, AX = mybir.AluOpType, mybir.ActivationFunctionType, mybir.AxisListType
    ds = bass.ds

    typed = [nc.dram_tensor(f"typed_table{i}", [NP * K, 3 * H], bf16) for i in range(2)]
    gin1_table = nc.dram_tensor("gin1_table", [NP, 3 * H], bf16)
    gin2_table = nc.dram_tensor("gin2_table", [NP, 3 * HID], bf16)
    gcn_table = nc.dram_tensor("gcn_table", [NP, 3 * H], bf16)
    sage_table = nc.dram_tensor("sage_table", [NP, 3 * H], bf16)
    tables = [typed[0], typed[1], typed[0], typed[1], gin1_table, gin2_table, gcn_table, sage_table]

    def width(p):
        return HID if p == GIN2 else H

    ctx = ExitStack()
    with ctx:
        def sb(name, shape, dt):
            return ctx.enter_context(nc.sbuf_tensor(name, shape, dt))

        def bank(name):
            return ctx.enter_context(nc.psum_tensor(name, [P, 512], fp32))

        def sem(name):
            return ctx.enter_context(nc.semaphore(name))

        x_all = sb("x_all", [P, NT, H], fp32)
        h_all = sb("h_all", [P, NT, H], fp32)
        big = sb("big", [P, NT * P], fp32)
        ring = sb("ring", [P, RING * 3 * H], bf16)
        onehot = sb("onehot", [P, max(OHS, 3 * OHS_W) * B * P], bf16)
        onehot_edge = sb("onehot_edge", [P, 3 * B * P], bf16)
        typed_idx = sb("typed_idx", [P, TP], i32)
        src_idx = sb("src_idx", [P, TP], i32)
        dst_id = sb("dst_id", [P, TP], i16)
        w_f = sb("w_f", [P, TP], fp32)
        idx_stage = sb("idx_stage", [P, 2, BLOCK], i32)
        zeros = sb("zeros", [P, 3 * HID], bf16)
        zero_row = sb("zero_row", [P, H], fp32)
        ones_bf = sb("ones_bf", [P, 1], bf16)
        ones_row = sb("ones_row", [1, P], fp32)
        ones_mean = sb("ones_mean", [P, P], fp32)
        eps_col = sb("eps_col", [P, 1], fp32)
        iota_row = sb("iota_row", [P, P], fp32)
        iota_col = sb("iota_col", [P, 1], fp32)
        bound_col = sb("bound_col", [P, 1], fp32)
        ident = sb("ident", [P, P], fp32)
        pick_last = sb("pick_last", [P, NT], fp32)
        mask_last = sb("mask_last", [P, 1], fp32)
        first_ids = sb("first_ids", [P, P, B], i16)
        node_ids = sb("node_ids", [P, P, B], i16)
        matches = sb("matches", [P, P, B], bf16)
        open_col = sb("open_col", [P, 1], fp32)
        first_open = sb("first_open", [1, NT + 2], i32)
        ahead_end = sb("ahead_end", [1, NT + 1], i32)
        count = sb("count", [P, NT], fp32)
        inv_count = sb("inv_count", [P, NT], fp32)
        deg_rsqrt = sb("deg_rsqrt", [P, NT], fp32)
        agg_sum = sb("agg_sum", [P, HID], fp32)
        aggT = sb("aggT", [H + 1, P], fp32)
        aggT_wide = sb("aggT_wide", [P, P], fp32)
        hT_cur = sb("hT_cur", [H + 1, P], fp32)
        hT_new = sb("hT_new", [H + 1, P], fp32)
        gates = sb("gates", [P, 2 * H], fp32)
        cand = sb("cand", [P, H], fp32)
        cand_act = sb("cand_act", [P, H], fp32)
        diff = sb("diff", [P, H], fp32)
        row_new = sb("row_new", [P, HID], fp32)
        y_row = sb("y_row", [P, H], fp32)
        v_row = sb("v_row", [P, H], fp32)
        o_row = sb("o_row", [P, H], fp32)
        out_row = sb("out_row", [P, H], fp32)
        uT = sb("uT", [P, P], fp32)
        rest = sb("rest", [P, K * H], fp32)
        stage = sb("stage", [P, K, 3 * H], bf16)
        stats6 = sb("stats6", [P, nc.vector.BN_STATS_DIM], fp32)
        moments = sb("moments", [P, 2], fp32)
        std = sb("std", [P, NT], fp32)
        rstd = sb("rstd", [P, 1], fp32)
        typed_w = sb("typed_w", [H + 1, K * H], fp32)
        gate_in_w = sb("gate_in_w", [H + 1, 4 * H], fp32)
        gate_h_w = sb("gate_h_w", [H + 1, 4 * H], fp32)
        raw_w = sb("raw_w", [P, 8, H], fp32)
        w1a = sb("w1a", [H, HID], fp32)
        w1b = sb("w1b", [HID, HID], fp32)
        w2a = sb("w2a", [HID, HID], fp32)
        w2b = sb("w2b", [HID, H], fp32)
        b1a_col = sb("b1a_col", [HID, 1], fp32)
        b2a_col = sb("b2a_col", [HID, 1], fp32)
        rows = sb("rows", [1, HID + 3 * H], fp32)
        b1b_row, b2b_row = rows[0:1, 0:HID], rows[0:1, HID:HID + H]
        b_self_row, b_neigh_row = rows[0:1, HID + H:HID + 2 * H], rows[0:1, HID + 2 * H:HID + 3 * H]
        gcn_w = sb("gcn_w", [H, H], fp32)
        gcn_b_all = sb("gcn_b_all", [P, H], fp32)
        gamma_all = sb("gamma_all", [P, H], fp32)
        beta_all = sb("beta_all", [P, H], fp32)
        self_wT = sb("self_wT", [H, H], fp32)
        neigh_wT = sb("neigh_wT", [H, H], fp32)
        mean_all = sb("mean_all", [P, H], fp32)
        var_all = sb("var_all", [P, H], fp32)
        ln_sum = sb("ln_sum", [P, NT], fp32)
        ln_rstd = sb("ln_rstd", [P, NT], fp32)
        mean_last = sb("mean_last", [P, P], fp32)

        lin = h_all[:, :, :].rearrange("p d f -> p (d f)")[:, 0:3 * TP].rearrange("p (a n) -> p a n", a=3)
        src_lin, dst_lin, typed_lin = lin[:, 0, :], lin[:, 1, :], lin[:, 2, :]
        raw_src, raw_dst, raw_type = [t.bitcast(i32) for t in (src_lin, dst_lin, typed_lin)]
        w_lin = onehot[:, :].bitcast(fp32)[:, TP // B + TP:TP // B + 2 * TP]
        featT = big[0:H, :]
        gin_h = big[:, :].rearrange("p (d f) -> p d f", f=HID)
        squares = big[:, 0:NT * H]
        w_left = big[:, NT * H:NT * H + TP]
        w_parts = big[:, NT * H + TP:NT * H + TP + 3 * TP // 2].bitcast(bf16).rearrange("p (a n) -> p a n", a=3)
        below = onehot[0:NT, :].bitcast(fp32)[:, 0:TP // B]
        ring_stage = ring[:, 0:4 * CH * 3 * H].rearrange("p (b d f) -> p b d f", b=4, d=CH)
        dst_f = onehot[:, :].bitcast(fp32)[:, TP // B:TP // B + TP]
        ring_f = ring[:, :].bitcast(fp32)
        first_stage = ring[:, 0:FS * PB * K * 3 * H].rearrange("p (b n) -> p b n", b=FS)
        at_rest = FS * PB * K * 3 * H // 2
        first_rest = ring_f[:, at_rest:at_rest + 2 * PB * K * H].rearrange("p (b n) -> p b n", b=2)
        at_x = at_rest + 2 * PB * K * H
        first_x = ring_f[:, at_x:at_x + 2 * (PB + 1) * H].rearrange("p (b n) -> p b n", b=2)
        at_T = at_x + 2 * (PB + 1) * H
        firstT = ring_f[0:H + 1, at_T:at_T + 2 * PB * P].rearrange("p (b n) -> p b n", b=2)

        ps_agg, ps_count, ps_T, ps_gates = bank("ps_agg"), bank("ps_count"), bank("ps_T"), bank("ps_gates")
        ps_typed, ps_u, ps_v, ps_T2 = bank("ps_typed"), bank("ps_u"), bank("ps_v"), bank("ps_T2")

        loaded = sem("loaded")
        edges_loaded = sem("edges_loaded")
        x_loaded = sem("x_loaded")
        state_loaded = sem("state_loaded")
        pads_set = sem("pads_set")
        consts_made = sem("consts_made")
        dve_consts = sem("dve_consts")
        w_turned = sem("w_turned")
        w_copied = sem("w_copied")
        edges_linear = sem("edges_linear")
        edges_turned = sem("edges_turned")
        edges_copied = sem("edges_copied")
        last_dst = sem("last_dst")
        open_counted = sem("open_counted")
        open_turned = sem("open_turned")
        open_ready = sem("open_ready")
        idx_staged = [sem(f"idx_staged{i}") for i in range(2)]
        pool_go = sem("pool_go")
        dve_go = sem("dve_go")
        group_landed = [sem(f"group_landed{i}") for i in range(RING // GROUP)]
        gathered = sem("gathered")
        batch_used = sem("batch_used")
        onehot_ready = sem("onehot_ready")
        edge_ready = sem("edge_ready")
        first_copied = sem("first_copied")
        firstT_ready = sem("firstT_ready")
        firstT_copied = sem("firstT_copied")
        first_typed = sem("first_typed")
        first_hi = sem("first_hi")
        first_left = sem("first_left")
        first_mid = sem("first_mid")
        first_lo = sem("first_lo")
        first_written = [sem(f"first_written{i}") for i in range(FS)]
        first_kept = sem("first_kept")
        agg_ready = sem("agg_ready")
        sum_ready = sem("sum_ready")
        aggT_ready = sem("aggT_ready")
        aggT_copied = sem("aggT_copied")
        hT_cur_ready = sem("hT_cur_ready")
        gates_ready = sem("gates_ready")
        sig_ready = sem("sig_ready")
        cand_ready = sem("cand_ready")
        tanh_ready = sem("tanh_ready")
        row_ready = sem("row_ready")
        rowT_ready = sem("rowT_ready")
        rowT_copied = sem("rowT_copied")
        typed_ready = sem("typed_ready")
        source_ready = sem("source_ready")
        hi_ready = sem("hi_ready")
        rest_ready = sem("rest_ready")
        mid_ready = sem("mid_ready")
        lo_ready = sem("lo_ready")
        table_written = sem("table_written")
        u_ready = sem("u_ready")
        u_copied = sem("u_copied")
        v_ready = sem("v_ready")
        v_copied = sem("v_copied")
        var_ready = sem("var_ready")
        std_ready = sem("std_ready")
        o_ready = sem("o_ready")
        o_biased = sem("o_biased")
        relu_done = sem("relu_done")
        deg_ready = sem("deg_ready")
        deg_root = sem("deg_root")
        bn_mean = sem("bn_mean")
        bn_centred = sem("bn_centred")
        bn_squared = sem("bn_squared")
        bn_var = sem("bn_var")
        bn_var_copied = sem("bn_var_copied")
        bn_std = sem("bn_std")
        bn_scale = sem("bn_scale")
        ch_scaled = sem("ch_scaled")
        ch_centred = sem("ch_centred")
        ch_squared = sem("ch_squared")
        ch_var = sem("ch_var")
        ch_std = sem("ch_std")
        ch_done = sem("ch_done")
        ch_hi = sem("ch_hi")
        ch_rest = sem("ch_rest")
        ch_mid = sem("ch_mid")
        ch_lo = sem("ch_lo")
        sage_written = [sem(f"sage_written{i}") for i in range(4)]
        x_cur_ready = sem("x_cur_ready")
        xT_ready = sem("xT_ready")
        xT_copied = sem("xT_copied")
        out_ready = sem("out_ready")
        out_written = sem("out_written")

        block = ctx.enter_context(nc.Block())

        EDGE_ROWS = E // TP
        EDGE_REST = E - EDGE_ROWS * TP
        EDGE_LOADS = 4 * 3
        LOADS = 25
        ALL_LOADED = 16 * LOADS

        @block.sync
        def _(sp):
            def load_x(to, done):
                sp.dma_start(to[:, 0:NT - 1, :],
                             x[0:(NT - 1) * P, :].rearrange("(d p) f -> p d f", p=P)).then_inc(done, 16)
                sp.dma_start(to[0:LAST, NT - 1, :], x[(NT - 1) * P:N, :]).then_inc(done, 16)

            sp.wait_ge(pads_set, 1)
            load_x(x_all, x_loaded)
            sp.wait_ge(pads_set, 2)
            for a, t in ((0, src), (1, dst), (2, edge_type), (3, edge_weight)):
                to = (raw_src, raw_dst, raw_type, w_lin)[a]
                for r0, r1 in ((0, 112), (112, EDGE_ROWS)):
                    sp.dma_start(to[r0:r1, :], t[r0 * TP:r1 * TP].rearrange("(p n) -> p n", n=TP)
                                 ).then_inc(edges_loaded, 16)
                sp.dma_start(to[EDGE_ROWS:EDGE_ROWS + 1, 0:EDGE_REST],
                             t[EDGE_ROWS * TP:E].rearrange("(p n) -> p n", p=1)).then_inc(edges_loaded, 16)
            for p in range(PASSES):
                idx = typed_idx if p < STEPS else src_idx

                if p == 0:
                    def store_first(b, q):
                        sp.wait_ge(first_lo, b + 1)
                        sp.dma_start(typed[0].ap().rearrange("(n k) f -> n (k f)", k=K)[ds(b * PB * P, PB * P), :]
                                     .rearrange("(t p) f -> p t f", p=P),
                                     first_stage[:, q, :].rearrange("p (t f) -> p t f", t=PB)
                                     ).then_inc(first_written[q], 16)

                    def store_some(a, b):
                        with sp.Fori(a, b) as i:
                            for q in range(FS):
                                store_first(i * FS + q, q)

                    store_some(0, EDGES_AT)
                    sp.wait_ge(edges_copied, TR)
                    sp.dma_start(h_all[:, :, :], x_all[:, :, :]).then_inc(state_loaded, 16)
                    store_some(EDGES_AT, NPB // FS)
                    store_first(NPB - 1, 0)

                def stage_block(b, half):
                    sp.dma_start(idx_stage[:, half, :], idx[:, ds(b * BLOCK, BLOCK)]
                                 ).then_inc(idx_staged[half], 16)

                def relay(i, g):
                    sp.wait_ge(group_landed[g], (i + 1 + ROUNDS * p) * 16 * GROUP)
                    sp.sem_inc(gathered, GROUP // B)

                stage_block(0, 0)
                stage_block(1, 1)
                half = RING // GROUP // 2
                with sp.Fori(0, ROUNDS - 1) as i:
                    for g in range(half):
                        relay(i, g)
                    stage_block(i * 2 + 2, 0)
                    for g in range(half, 2 * half):
                        relay(i, g)
                    stage_block(i * 2 + 3, 1)
                for g in range(2 * half):
                    relay(ROUNDS - 1, g)
                if p == GCN:
                    for c in range(NCH):
                        sp.wait_ge(ch_lo, c + 1)
                        sp.dma_start(sage_table.ap()[c * CH * P:(c + 1) * CH * P, :]
                                     .rearrange("(d p) f -> p d f", p=P), ring_stage[:, c % 4]
                                     ).then_inc(sage_written[c % 4], 16)

        @block.gpsimd
        def _(pool):
            nc.gpsimd.memset(x_all[:, NT - 1, :], 0.0)
            nc.gpsimd.memset(gate_in_w[:, 3 * H:4 * H], 0.0)
            nc.gpsimd.memset(gate_h_w[:, 2 * H:3 * H], 0.0).then_inc(pads_set, 1)
            nc.gpsimd.memset(raw_src, 0)
            nc.gpsimd.memset(raw_dst, NO_NODE)
            nc.gpsimd.memset(raw_type, 0)
            nc.gpsimd.memset(w_lin, 0.0).then_inc(pads_set, 1)
            nc.gpsimd.iota(iota_row[:, :], pattern=[[1, P]], base=0, channel_multiplier=0,
                           allow_small_or_imprecise_dtypes=True)
            nc.gpsimd.iota(iota_col[:, :], pattern=[[0, 1]], base=0, channel_multiplier=1,
                           allow_small_or_imprecise_dtypes=True)
            nc.gpsimd.iota(bound_col[:, :], pattern=[[0, 1]], base=P, channel_multiplier=P,
                           allow_small_or_imprecise_dtypes=True)
            nc.gpsimd.memset(zeros[:, :], 0.0)
            nc.gpsimd.memset(zero_row[:, :], 0.0)
            nc.gpsimd.memset(ones_bf[:, :], 1.0)
            nc.gpsimd.memset(ones_row[:, :], 1.0)
            nc.gpsimd.memset(ones_mean[:, :], 1.0 / N)
            nc.gpsimd.memset(eps_col[:, :], EPS)
            nc.gpsimd.memset(first_open[:, 0:1], 0)
            nc.gpsimd.iota(first_ids[:, :, :], pattern=[[1, P], [0, B]], base=-P, channel_multiplier=0)
            nc.gpsimd.memset(first_x[:, :, :], 0.0)
            nc.gpsimd.memset(agg_sum[:, :], 0.0)
            nc.gpsimd.memset(row_new[:, :], 0.0)
            pool.drain()
            for t in (aggT, hT_cur, hT_new):
                nc.gpsimd.memset(t[H:H + 1, :], 1.0)
            nc.gpsimd.memset(firstT[H:H + 1, :, :], 1.0)
            pool.drain().then_inc(consts_made, 1)

            pool.wait_ge(x_loaded, 32)

            def copy_first(b, q):
                nc.gpsimd.tensor_copy(first_x[:, q, 0:PB * H],
                                      x_all[:, ds(b * PB, PB), :].rearrange("p t f -> p (t f)")
                                      ).then_inc(first_copied, 1)

            def keep_first(b, q):
                pool.wait_ge(firstT_copied, b + 1)
                pool.sem_inc(pool_go, 1)
                nc.gpsimd.tensor_copy(featT[:, ds(b * PB * P, PB * P)], firstT[0:H, q, :]).then_inc(first_kept, 1)

            copy_first(0, 0)
            copy_first(1, 1)
            with pool.Fori(0, NPB // 2 - 1) as i:
                for q in range(2):
                    pool.wait_ge(firstT_ready, i * 2 + q + 1)
                    pool.sem_inc(pool_go, 1)
                    copy_first(i * 2 + q + 2, q)
                    keep_first(i * 2 + q, q)
            pool.wait_ge(firstT_ready, NPB - 2)
            copy_first(NPB - 1, 0)
            for b in range(NPB - 3, NPB):
                keep_first(b, b % 2)
            pool.wait_ge(first_kept, NPB)

            for p in range(PASSES):
                F3 = 3 * width(p)
                slots = RING * H // width(p)
                if p == 0:
                    for q in range(FS):
                        pool.wait_ge(first_written[q], 16 * len(range(q, NPB, FS)))
                elif p < SAGE:
                    pool.wait_ge(table_written, 16 * NT * p + STORED)
                else:
                    for i in range(4):
                        pool.wait_ge(sage_written[i], 16 * len(range(i, NCH, 4)))
                pool.sem_inc(pool_go, 1)
                with pool.Fori(0, ROUNDS) as i:
                    for t in range(RING):
                        if t % BLOCK == 0:
                            pool.wait_ge(idx_staged[t // BLOCK], (i + 1 + ROUNDS * p) * 16)
                            pool.sem_inc(pool_go, 1)
                        if t % GROUP == 0:
                            pool.wait_ge(batch_used, i * (RING // B)
                                         + (FULL * p + CREDIT + (t + GROUP - slots) // B))
                            pool.sem_inc(pool_go, 1)
                        s = t % slots
                        pool.indirect_dma_start(
                            out=ring[:, s * F3:(s + 1) * F3], out_offset=None, in_=tables[p].ap(),
                            in_offset=bass.IndirectOffsetOnAxis(
                                ap=idx_stage[:, t // BLOCK, t % BLOCK:t % BLOCK + 1], axis=0)
                        ).then_inc(group_landed[t // GROUP], 16)

                if p == GCN:
                    def rest_of(c):
                        return squares.rearrange("p (d f) -> p d f", f=H)[:, c * CH:(c + 1) * CH, :]

                    pool.wait_ge(bn_scale, 1)
                    for c in range(NCH):
                        hc = h_all[:, c * CH:(c + 1) * CH, :]
                        nc.gpsimd.tensor_tensor(hc, hc, gamma_all[:, :].rearrange("p (o f) -> p o f", o=1)
                                                .to_broadcast([P, CH, H]), ALU.mult).then_inc(ch_scaled, 1)
                    for c in range(NCH + 1):
                        if c < NCH:
                            pool.wait_ge(ch_hi, c + 1)
                            nc.gpsimd.tensor_tensor(rest_of(c), x_all[:, c * CH:(c + 1) * CH, :],
                                                    ring_stage[:, c % 4, :, 0:H], ALU.subtract).then_inc(ch_rest, 1)
                        if c >= 1:
                            st = ring_stage[:, (c - 1) % 4]
                            pool.wait_ge(ch_mid, c)
                            nc.gpsimd.tensor_tensor(st[:, :, 2 * H:3 * H], rest_of(c - 1), st[:, :, H:2 * H],
                                                    ALU.subtract).then_inc(ch_lo, 1)

        @block.tensor
        def _(pe):
            pe.wait_ge(loaded, ALL_LOADED)
            pe.wait_ge(dve_consts, 1)
            nc.tensor.transpose(ps_T[0:H, 0:P], raw_w[:, 0, :], ident[:, :])
            nc.tensor.transpose(ps_T[0:H, P:2 * P], raw_w[:, 1, :], ident[:, :])
            nc.tensor.transpose(ps_T[0:H, 2 * P:3 * P], raw_w[:, 2, :], ident[:, :])
            nc.tensor.transpose(ps_T[0:H, 3 * P:3 * P + H], raw_w[0:H, 3, :], ident[0:H, 0:H])
            nc.tensor.transpose(ps_gates[0:H, 0:P], raw_w[:, 4, :], ident[:, :])
            nc.tensor.transpose(ps_gates[0:H, P:P + H], raw_w[0:H, 5, :], ident[0:H, 0:H])
            nc.tensor.transpose(ps_gates[0:H, 2 * P:2 * P + H], raw_w[0:H, 6, :], ident[0:H, 0:H])
            nc.tensor.transpose(ps_gates[0:H, 3 * P:3 * P + H], raw_w[0:H, 7, :], ident[0:H, 0:H]
                                ).then_inc(w_turned, 1)
            pe.wait_ge(w_copied, 1)

            def typed_rows(p, d):
                pe.wait_ge(row_ready, NT * p + 1 + d)
                nc.tensor.transpose(ps_T2[:, 0:P], row_new[:, :], ident[:, :]).then_inc(rowT_ready, 1)
                pe.wait_ge(rowT_copied, NT * p + 1 + d)
                nc.tensor.matmul(ps_typed[:, 0:K * H], hT_new[:, :], typed_w[:, :],
                                 start=True, stop=True).then_inc(typed_ready, 1)

            first_T, first_M = (ps_T, ps_T2), (ps_typed, ps_gates)

            def turn_first(b, q, warm):
                pe.wait_ge(first_copied, b + 1)
                if warm:
                    pe.wait_ge(firstT_copied, b - 1)
                for t in range(PB):
                    last = nc.tensor.transpose(first_T[q][:, t * P:(t + 1) * P],
                                               first_x[:, q, t * H:t * H + P], ident[:, :])
                last.then_inc(firstT_ready, 1)

            def type_first(b, q, warm):
                pe.wait_ge(firstT_copied, b + 1)
                if warm:
                    pe.wait_ge(first_left, b - 1)
                for t in range(PB):
                    last = nc.tensor.matmul(first_M[q][:, t * K * H:(t + 1) * K * H], firstT[:, q, t * P:(t + 1) * P],
                                            typed_w[:, :], start=True, stop=True)
                last.then_inc(first_typed, 1)

            def lay_out_edges():
                pe.wait_ge(edges_linear, 1)
                turn = [ps_u, ps_v]
                for j in range(TR):
                    if j >= 2:
                        pe.wait_ge(edges_copied, j - 1)
                    for a, t in enumerate((src_lin, typed_lin, dst_lin, w_lin)):
                        last = nc.tensor.transpose(turn[j % 2][:, a * P:(a + 1) * P], t[:, j * P:(j + 1) * P],
                                                   ident[:, :])
                    last.then_inc(edges_turned, 1)

            turn_first(0, 0, False)
            turn_first(1, 1, False)
            for b in range(2):
                turn_first(b + 2, b, True)
                type_first(b, b, False)
            for lo, hi in ((1, 2 * EDGES_AT), (2 * EDGES_AT, NPB // 2 - 1)):
                with pe.Fori(lo, hi) as i:
                    for q in range(2):
                        turn_first(i * 2 + q + 2, q, True)
                        type_first(i * 2 + q, q, True)
                if hi == 2 * EDGES_AT:
                    lay_out_edges()
            turn_first(NPB - 1, 0, True)
            type_first(NPB - 3, 0, True)
            type_first(NPB - 2, 1, True)
            type_first(NPB - 1, 0, True)
            pe.wait_ge(edges_copied, TR)
            nc.tensor.matmul(ps_agg[0:NT, 0:TP // B], pick_last[:, :],
                             dst_f[:, :].rearrange("e (g b) -> e b g", b=B)[:, B - 1, :],
                             start=True, stop=True).then_inc(last_dst, 1)
            pe.wait_ge(open_counted, 1)
            nc.tensor.matmul(ps_count[0:1, 0:NT], open_col[0:NT, :], ident[0:NT, 0:NT],
                             start=True, stop=True).then_inc(open_turned, 1)
            pe.wait_ge(open_ready, 1)

            for p in range(PASSES):
                F3 = 3 * width(p)
                slots = RING * H // width(p)
                parts = 3 if p == SAGE else 1

                oh_slots = OHS_W if p == SAGE else OHS

                def batch_product(onehots, g, last):
                    row0 = pe.snap((g % (slots // B)) * (B * F3))
                    for k in range(parts * B):
                        end = last and k == parts * B - 1
                        oh = onehots(k // B).rearrange("p (n b) -> p b n", b=B)[:, k % B, :]
                        if p == 0:
                            nc.tensor.matmul(ps_count[:, 0:1], oh, ones_bf[:, :], start=False, stop=end)
                        ins = nc.tensor.matmul(ps_agg[:, 0:F3], oh, ring[:, ds(row0 + (k % B) * F3, F3)],
                                               start=False, stop=end)
                    return ins

                def node_tile(d):
                    lo = pe.value_load(first_open[0:1, ds(d, 1)], min_val=0, max_val=FULL)
                    hi = pe.value_load(first_open[0:1, ds(d + 1, 1)], min_val=0, max_val=FULL)
                    nc.tensor.matmul(ps_agg[:, 0:F3], zeros[:, 0:P], zeros[:, 0:F3], start=True, stop=False)
                    if p == 0:
                        nc.tensor.matmul(ps_count[:, 0:1], zeros[:, 0:P], zeros[:, 0:1], start=True, stop=False)
                    with pe.If(lo < hi):
                        with pe.Fori(lo, hi) as g:
                            pe.wait_ge(onehot_ready, g + (1 + FULL * p))
                            pe.wait_ge(gathered, g + (1 + TP // B * p))
                            slot = pe.snap((g % oh_slots) * (parts * B * P))
                            batch_product(lambda a: onehot[:, ds(slot + a * (B * P), B * P)], g, False
                                          ).then_inc(batch_used, 1)
                    pe.wait_ge(edge_ready, d + (1 + (NT + 1) * p))
                    pe.wait_ge(gathered, hi + (1 + TP // B * p))
                    batch_product(lambda a: onehot_edge[:, a * B * P:(a + 1) * B * P], hi, True).then_inc(agg_ready, 1)
                    here = NT * p + 1
                    if p == SAGE:
                        pe.wait_ge(x_cur_ready, d + 1)
                        nc.tensor.transpose(ps_T2[:, 0:P], row_new[:, :], ident[:, :]).then_inc(xT_ready, 1)
                    pe.wait_ge(sum_ready, here + d)
                    nc.tensor.transpose(ps_T[:, 0:P], agg_sum[:, :], ident[:, :]).then_inc(aggT_ready, 1)
                    if p < STEPS:
                        pe.wait_ge(hT_cur_ready, here + d)
                        nc.tensor.matmul(ps_gates[:, 0:4 * H], hT_cur[:, :], gate_h_w[:, :],
                                         start=True, stop=False)
                        pe.wait_ge(aggT_copied, here + d)
                        nc.tensor.matmul(ps_gates[:, 0:4 * H], aggT[:, :], gate_in_w[:, :],
                                         start=False, stop=True).then_inc(gates_ready, 1)
                        if p < STEPS - 1:
                            typed_rows(p, d)
                    elif p in (GIN1, GIN2):
                        base = NT * (p - GIN1) + 1
                        pe.wait_ge(aggT_copied, here + d)
                        if p == GIN1:
                            nc.tensor.matmul(ps_u[:, 0:P], w1a[:, :], aggT[0:H, :],
                                             start=True, stop=True).then_inc(u_ready, 1)
                        else:
                            nc.tensor.matmul(ps_u[:, 0:P], w2a[:, :], aggT_wide[:, :],
                                             start=True, stop=True).then_inc(u_ready, 1)
                        pe.wait_ge(u_copied, base + d)
                        O = HID if p == GIN1 else H
                        nc.tensor.matmul(ps_v[:, 0:O], uT[:, :], (w1b if p == GIN1 else w2b)[:, :],
                                         start=True, stop=False)
                        nc.tensor.matmul(ps_v[:, 0:O], ones_row[:, :], b1b_row if p == GIN1 else b2b_row,
                                         start=False, stop=True).then_inc(v_ready, 1)
                    elif p == GCN:
                        pe.wait_ge(aggT_copied, here + d)
                        nc.tensor.matmul(ps_u[:, 0:H], aggT[0:H, :], gcn_w[:, :],
                                         start=True, stop=True).then_inc(o_ready, 1)
                        pe.wait_ge(relu_done, d + 1)
                        last_tile = isinstance(d, int)
                        if not last_tile:
                            nc.tensor.matmul(ps_count[:, 0:H], ones_mean[:, :],
                                             h_all[:, ds(d, 1), :].rearrange("p o f -> p (o f)"),
                                             start=False, stop=False)
                        else:
                            nc.tensor.matmul(ps_count[:, 0:H], mean_last[:, :], h_all[:, d, :],
                                             start=False, stop=True).then_inc(bn_mean, 1)
                    else:
                        pe.wait_ge(xT_copied, d + 1)
                        nc.tensor.matmul(ps_v[:, 0:H], hT_new[0:H, :], self_wT[:, :], start=True, stop=False)
                        nc.tensor.matmul(ps_v[:, 0:H], ones_row[:, :], b_self_row, start=False, stop=False)
                        nc.tensor.matmul(ps_v[:, 0:H], ones_row[:, :], b_neigh_row, start=False, stop=False)
                        pe.wait_ge(aggT_copied, here + d)
                        nc.tensor.matmul(ps_v[:, 0:H], aggT[0:H, :], neigh_wT[:, :],
                                         start=False, stop=True).then_inc(o_ready, 1)

                if p == GCN:
                    nc.tensor.matmul(ps_count[:, 0:H], ones_mean[:, :], zero_row[:, :], start=True, stop=False)
                if p < GCN:
                    with pe.Fori(0, NT) as d:
                        node_tile(d)
                else:
                    with pe.Fori(0, NT - 1) as d:
                        node_tile(d)
                    node_tile(NT - 1)

                if p == GCN:
                    cols, part = CH * H, CH * H // 2
                    for c in range(NCH):
                        pe.wait_ge(bn_squared, c + 1)
                        for k in range(2):
                            last = nc.tensor.matmul(ps_u[:, 0:part], ones_mean[:, :],
                                                    squares[:, c * cols + k * part:c * cols + (k + 1) * part],
                                                    start=c + k == 0, stop=c == NCH - 1 and k == 1)
                    last.then_inc(bn_var, 1)

        @block.scalar
        def _(act):
            pieces = [
                (raw_w[:, 0:2, :], g_W.rearrange("(c k) h d -> (k h) c d", c=2)),
                (raw_w[:, 2, :], g_w_ih[0:P, :]), (raw_w[0:H, 3, :], g_w_ih[P:3 * H, :]),
                (raw_w[:, 4, :], g_w_hh[0:P, :]), (raw_w[0:H, 5, :], g_w_hh[P:3 * H, :]),
                (raw_w[0:H, 6, :], W_self), (raw_w[0:H, 7, :], W_neigh),
                (typed_w[H:H + 1, :], g_b.rearrange("(o k) h -> o (k h)", o=1)),
                (gate_in_w[H:H + 1, 0:3 * H], g_b_ih.rearrange("(o n) -> o n", o=1)),
                (gate_h_w[H:H + 1, 0:2 * H], g_b_hh[0:2 * H].rearrange("(o n) -> o n", o=1)),
                (gate_h_w[H:H + 1, 3 * H:4 * H], g_b_hh[2 * H:3 * H].rearrange("(o n) -> o n", o=1)),
                (w1a[:, :], W1a), (w1b[:, :], W1b), (w2a[:, :], W2a), (w2b[:, :], W2b),
                (b1a_col[:, :], b1a.rearrange("(n o) -> n o", o=1)),
                (b2a_col[:, :], b2a.rearrange("(n o) -> n o", o=1)),
                (rows[0:1, 0:HID], b1b.rearrange("(o n) -> o n", o=1)),
                (rows[0:1, HID:HID + H], b2b.rearrange("(o n) -> o n", o=1)),
                (rows[0:1, HID + H:HID + 2 * H], b_self.rearrange("(o n) -> o n", o=1)),
                (rows[0:1, HID + 2 * H:HID + 3 * H], b_neigh.rearrange("(o n) -> o n", o=1)),
                (gcn_w[:, :], gcn_W),
            ]
            act.sem_inc(table_written, STORED)
            act.wait_ge(pads_set, 1)
            for to, frm in pieces:
                act.dma_start(to, frm).then_inc(loaded, 16)
            for to, frm in ((gcn_b_all, gcn_b), (gamma_all, gamma), (beta_all, beta)):
                act.dma_start(to[:, :], frm.rearrange("(o n) -> o n", o=1).to_broadcast([P, H])
                              ).then_inc(loaded, 16)
            assert len(pieces) + 3 == LOADS

            def split_and_store(p, d, source, groups, W, table_rows):
                at = NT * p + d
                hi, mid = stage_parts(groups, W)[0:2]
                act.wait_ge(table_written, at * 16 + STORED)
                act.activation(hi, source, ACT.Copy).then_inc(hi_ready, 1)
                act.wait_ge(rest_ready, at + 1)
                act.activation(mid, rest[:, 0:groups * W].rearrange("p (k w) -> p k w", k=groups), ACT.Copy
                               ).then_inc(mid_ready, 1)
                act.wait_ge(lo_ready, at + 1)
                act.dma_start(table_rows, stage_flat[:, 0:3 * W * groups]).then_inc(table_written, 16)

            stage_flat = stage[:, :, :].rearrange("p k n -> p (k n)")

            def stage_parts(groups, W):
                v = stage_flat[:, 0:3 * W * groups].rearrange("p (k a w) -> p k a w", k=groups, a=3)
                return [v[:, :, a, :] for a in range(3)]

            def typed_rows(p, d):
                at = NT * p + 1
                act.wait_ge(rowT_ready, at + d)
                act.activation(hT_new[0:H, :], ps_T2[0:H, 0:P], ACT.Copy).then_inc(rowT_copied, 1)
                act.activation(featT[:, ds(d * P, P)], ps_T2[0:H, 0:P], ACT.Copy)
                act.wait_ge(typed_ready, at + d)
                to = typed[(p + 1) % 2].ap().rearrange("(n k) f -> n (k f)", k=K)[ds(d * P, P), :]
                split_and_store(p, d, ps_typed[:, 0:K * H].rearrange("p (k w) -> p k w", k=K), K, H, to)

            first_T, first_M = (ps_T, ps_T2), (ps_typed, ps_gates)

            def first_part(t, a):
                return t.rearrange("p (k a w) -> p k a w", k=PB * K, a=3)[:, :, a, :]

            def copy_firstT(b, q, warm):
                act.wait_ge(firstT_ready, b + 1)
                if warm:
                    act.wait_ge(first_kept, b - 1)
                act.activation(firstT[0:H, q, :], first_T[q][0:H, 0:PB * P], ACT.Copy).then_inc(firstT_copied, 1)

            def hi_first(b, q, s, round_):
                act.wait_ge(first_typed, b + 1)
                if round_ is not None:
                    act.wait_ge(first_written[s], round_ * 16)
                act.activation(first_part(first_stage[:, s, :], 0),
                               first_M[q][:, :].rearrange("p (k w) -> p k w", w=H), ACT.Copy).then_inc(first_hi, 1)

            def mid_first(b, q, s):
                act.wait_ge(first_left, b + 1)
                act.activation(first_part(first_stage[:, s, :], 1),
                               first_rest[:, q, :].rearrange("p (k w) -> p k w", w=H), ACT.Copy
                               ).then_inc(first_mid, 1)

            copy_firstT(0, 0, False)
            copy_firstT(1, 1, False)
            for b in range(FS):
                hi_first(b, b % 2, b, None)
                copy_firstT(b + 2, b % 2, True)
                mid_first(b, b % 2, b)
            with act.Fori(1, NPB // FS) as i:
                for s in range(FS):
                    hi_first(i * FS + s, s % 2, s, i)
                    if s < FS - 1:
                        copy_firstT(i * FS + s + 2, s % 2, True)
                    else:
                        with act.If(i < NPB // FS - 1):
                            copy_firstT(i * FS + s + 2, s % 2, True)
                    mid_first(i * FS + s, s % 2, s)
            hi_first(NPB - 1, 0, 0, NPB // FS)
            mid_first(NPB - 1, 0, 0)

            def layernorm_root(k, d):
                act.wait_ge(var_ready, NT * k + 1 + d)
                act.activation(std[:, 0:1], moments[:, 1:2], ACT.Sqrt, bias=eps_col[:, :]).then_inc(std_ready, 1)

            for p in range(PASSES):
                here = NT * p + 1
                if p == 1:
                    act.wait_ge(deg_ready, 1)
                    act.activation(deg_rsqrt[:, :], std[:, :], ACT.Sqrt).then_inc(deg_root, 1)

                def node_tile(d):
                    if p < STEPS:
                        act.activation(hT_cur[0:H, :], featT[:, ds(d * P, P)], ACT.Copy
                                       ).then_inc(hT_cur_ready, 1)
                    if p == SAGE:
                        act.activation(row_new[:, 0:H], x_all[:, ds(d, 1), :].rearrange("p o f -> p (o f)"), ACT.Copy
                                       ).then_inc(x_cur_ready, 1)
                        act.wait_ge(xT_ready, d + 1)
                        act.activation(hT_new[0:H, :], ps_T2[0:H, 0:P], ACT.Copy).then_inc(xT_copied, 1)
                    act.wait_ge(aggT_ready, here + d)
                    if p == GIN2:
                        act.activation(aggT_wide[:, :], ps_T[:, 0:P], ACT.Copy).then_inc(aggT_copied, 1)
                    else:
                        act.activation(aggT[0:H, :], ps_T[0:H, 0:P], ACT.Copy).then_inc(aggT_copied, 1)
                    if p < STEPS:
                        act.wait_ge(gates_ready, here + d)
                        act.activation(gates[:, :], ps_gates[:, 0:2 * H], ACT.Tanh, scale=0.5
                                       ).then_inc(sig_ready, 1)
                        act.wait_ge(cand_ready, here + d)
                        act.activation(cand_act[:, :], cand[:, :], ACT.Tanh).then_inc(tanh_ready, 1)
                        if p < STEPS - 1:
                            typed_rows(p, d)
                        else:
                            layernorm_root(0, d)
                            act.wait_ge(source_ready, d + 1)
                            split_and_store(p, d, row_new[:, 0:H].rearrange("p (k w) -> p k w", k=1), 1, H,
                                            gin1_table.ap()[ds(d * P, P), :])
                    elif p in (GIN1, GIN2):
                        base = NT * (p - GIN1) + 1
                        act.wait_ge(u_ready, base + d)
                        act.activation(uT[:, :], ps_u[:, 0:P], ACT.Relu,
                                       bias=(b1a_col if p == GIN1 else b2a_col)[:, :]).then_inc(u_copied, 1)
                        act.wait_ge(v_ready, base + d)
                        if p == GIN1:
                            act.activation(row_new[:, :], ps_v[:, 0:HID], ACT.Relu).then_inc(v_copied, 1)
                            act.drain()
                            split_and_store(p, d, row_new[:, :].rearrange("p (k w) -> p k w", k=1), 1, HID,
                                            gin2_table.ap()[ds(d * P, P), :])
                        else:
                            act.activation(v_row[:, :], ps_v[:, 0:H], ACT.Relu).then_inc(v_copied, 1)
                            layernorm_root(1, d)
                            act.wait_ge(source_ready, NT + 1 + d)
                            split_and_store(p, d, row_new[:, 0:H].rearrange("p (k w) -> p k w", k=1), 1, H,
                                            gcn_table.ap()[ds(d * P, P), :])
                    elif p == GCN:
                        act.wait_ge(o_biased, d + 1)
                        act.activation(h_all[:, ds(d, 1), :].rearrange("p o f -> p (o f)"), o_row[:, :], ACT.Relu
                                       ).then_inc(relu_done, 1)
                    else:
                        layernorm_root(2, d)
                        act.wait_ge(out_ready, d + 1)
                        if isinstance(d, int):
                            act.dma_start(out[d * P:N, :], out_row[0:LAST, :]).then_inc(out_written, 16)
                        else:
                            act.dma_start(out[ds(d * P, P), :], out_row[:, :]).then_inc(out_written, 16)
                        act.wait_ge(out_written, d * 16 + 16)

                if p < GCN:
                    with act.Fori(0, NT) as d:
                        node_tile(d)
                else:
                    with act.Fori(0, NT - 1) as d:
                        node_tile(d)
                    node_tile(NT - 1)
                if p == SAGE:
                    act.wait_ge(out_written, 16 * NT)

                if p == GCN:
                    def chunk(c):
                        sq = squares.rearrange("p (d f) -> p d f", f=H)[:, c * CH:(c + 1) * CH, :]
                        return (h_all[:, c * CH:(c + 1) * CH, :], sq, x_all[:, c * CH:(c + 1) * CH, :],
                                ring_stage[:, c % 4])

                    for c in range(NCH):
                        hc, sq, xc, st = chunk(c)
                        act.wait_ge(bn_centred, c + 1)
                        act.activation(sq, hc, ACT.Square).then_inc(bn_squared, 1)
                    act.wait_ge(bn_var_copied, 1)
                    act.activation(var_all[:, :], var_all[:, :], ACT.Sqrt, bias=eps_col[:, :]).then_inc(bn_std, 1)

                    def square(c):
                        hc, sq, xc, st = chunk(c)
                        act.wait_ge(ch_centred, c + 1)
                        act.activation(sq, hc, ACT.Square).then_inc(ch_squared, 1)

                    def root(c):
                        act.wait_ge(ch_var, c + 1)
                        act.activation(std[:, c * CH:(c + 1) * CH], ln_rstd[:, c * CH:(c + 1) * CH], ACT.Sqrt,
                                       bias=eps_col[:, :], scale=1.0 / H).then_inc(ch_std, 1)

                    def high(c):
                        hc, sq, xc, st = chunk(c)
                        act.wait_ge(ch_done, c + 1)
                        if c >= 4:
                            act.wait_ge(sage_written[c % 4], 16)
                        act.activation(st[:, :, 0:H], xc, ACT.Copy).then_inc(ch_hi, 1)

                    def middle(c):
                        hc, sq, xc, st = chunk(c)
                        act.wait_ge(ch_rest, c + 1)
                        act.activation(st[:, :, H:2 * H], sq, ACT.Copy).then_inc(ch_mid, 1)

                    for c in range(NCH + 2):
                        if c < NCH:
                            square(c)
                        if 1 <= c <= NCH:
                            root(c - 1)
                            high(c - 1)
                        if c >= 2:
                            middle(c - 2)

        @block.vector
        def _(dve):
            dve.sem_inc(batch_used, CREDIT)
            dve.wait_ge(consts_made, 1)
            v = nc.vector
            v.tensor_scalar(ident[:, :], iota_row[:, :], iota_col[:, :], None, ALU.is_equal)
            v.tensor_scalar(pick_last[:, :], iota_col[:, :].to_broadcast([P, NT]), float(P - 1), None, ALU.is_equal)
            v.tensor_scalar(mask_last[:, :], iota_col[:, :], float(LAST), None, ALU.is_lt)
            dve.drain().then_inc(dve_consts, 1)
            v.tensor_scalar(mean_last[:, :], ones_mean[:, :], mask_last[:, :], None, ALU.mult)
            dve.wait_ge(loaded, ALL_LOADED)
            dve.wait_ge(w_turned, 1)
            v.tensor_copy(typed_w[0:H, :], ps_T[0:H, 0:2 * P])
            v.tensor_copy(gate_in_w[0:H, 0:3 * H], ps_T[0:H, 2 * P:2 * P + 3 * H])
            v.tensor_copy(gate_h_w[0:H, 0:2 * H], ps_gates[0:H, 0:2 * H])
            v.tensor_copy(gate_h_w[0:H, 3 * H:4 * H], ps_gates[0:H, 2 * H:3 * H])
            v.tensor_copy(self_wT[:, :], ps_gates[0:H, 2 * P:2 * P + H])
            v.tensor_copy(neigh_wT[:, :], ps_gates[0:H, 3 * P:3 * P + H]).then_inc(w_copied, 1)

            def first_part(t, a):
                return t.rearrange("p (k a w) -> p k a w", k=PB * K, a=3)[:, :, a, :]

            def rest_first(b, q, s):
                dve.wait_ge(first_hi, b + 1)
                v.tensor_tensor(first_rest[:, q, :].rearrange("p (k w) -> p k w", w=H),
                                (ps_typed, ps_gates)[q][:, :].rearrange("p (k w) -> p k w", w=H),
                                first_part(first_stage[:, s, :], 0), ALU.subtract).then_inc(first_left, 1)

            def lo_first(b, q, s):
                dve.wait_ge(first_mid, b + 1)
                v.tensor_tensor(first_part(first_stage[:, s, :], 2),
                                first_rest[:, q, :].rearrange("p (k w) -> p k w", w=H),
                                first_part(first_stage[:, s, :], 1), ALU.subtract).then_inc(first_lo, 1)

            def lay_out_edges():
                dve.wait_ge(edges_loaded, 16 * EDGE_LOADS)
                v.scalar_tensor_tensor(out=typed_lin, in0=raw_src, scalar=float(K), in1=raw_type,
                                       op0=ALU.mult, op1=ALU.add)
                v.tensor_copy(dst_lin, raw_dst)
                dve.drain()
                v.tensor_copy(src_lin, raw_src).then_inc(edges_linear, 1)
                turn = [ps_u, ps_v]
                for j in range(TR):
                    dve.wait_ge(edges_turned, j + 1)
                    for a, to in ((0, src_idx), (1, typed_idx), (2, dst_id), (2, dst_f), (3, w_f)):
                        last = v.tensor_copy(to[:, :].rearrange("e (p j) -> e j p", j=TR)[:, j, :],
                                             turn[j % 2][:, a * P:(a + 1) * P])
                    last.then_inc(edges_copied, 1)

            for lo, hi in ((0, EDGES_AT), (EDGES_AT, NPB // FS)):
                with dve.Fori(lo, hi) as i:
                    for s in range(FS):
                        rest_first(i * FS + s, s % 2, s)
                        lo_first(i * FS + s, s % 2, s)
                if hi == EDGES_AT:
                    lay_out_edges()
            rest_first(NPB - 1, 0, 0)
            lo_first(NPB - 1, 0, 0)
            dve.wait_ge(last_dst, 1)
            v.tensor_scalar(below, ps_agg[0:NT, 0:TP // B], bound_col[0:NT, :], None, ALU.is_lt)
            dve.drain()
            v.reduce_sum(open_col[0:NT, :], below, axis=AX.X).then_inc(open_counted, 1)
            dve.wait_ge(open_turned, 1)
            v.tensor_copy(first_open[0:1, 1:NT + 1], ps_count[0:1, 0:NT])
            v.tensor_copy(first_open[0:1, NT + 1:NT + 2], ps_count[0:1, NT - 1:NT])
            dve.drain()
            v.tensor_scalar(ahead_end[:, :], first_open[:, 0:NT + 1], float(AHEAD), None, ALU.add)
            dve.drain()
            v.tensor_tensor(ahead_end[:, :], ahead_end[:, :], first_open[:, 1:NT + 2], ALU.min)
            dve.drain().then_inc(open_ready, 1)
            dve.wait_ge(open_ready, 1)

            stage_flat = stage[:, :, :].rearrange("p k n -> p (k n)")

            def split(p, d, source, groups, W):
                at = NT * p + 1
                parts = stage_flat[:, 0:3 * W * groups].rearrange("p (k a w) -> p k a w", k=groups, a=3)
                r = rest[:, 0:groups * W].rearrange("p (k w) -> p k w", k=groups)
                dve.wait_ge(hi_ready, at + d)
                v.tensor_tensor(r, source, parts[:, :, 0, :], ALU.subtract).then_inc(rest_ready, 1)
                dve.wait_ge(mid_ready, at + d)
                v.tensor_tensor(parts[:, :, 2, :], r, parts[:, :, 1, :], ALU.subtract).then_inc(lo_ready, 1)

            def typed_rows(p, d):
                split(p, d, ps_typed[:, 0:K * H].rearrange("p (k w) -> p k w", k=K), K, H)

            def tile(t, d):
                return t[:, ds(d, 1), :].rearrange("p o f -> p (o f)")

            def layernorm(k, d, to):
                dve.drain()
                v.bn_stats(stats6[:, :], y_row[:, :])
                dve.drain()
                v.bn_aggr(moments[:, :], stats6[:, :]).then_inc(var_ready, 1)
                dve.wait_ge(std_ready, NT * k + 1 + d)
                v.reciprocal(rstd[:, :], std[:, 0:1])
                dve.drain()
                return v.tensor_scalar(to, y_row[:, :], moments[:, 0:1], rstd[:, :], ALU.subtract, ALU.mult)

            dve.wait_ge(x_loaded, 32)
            dve.wait_ge(state_loaded, 16)
            for p in range(PASSES):
                W = width(p)
                if p == 1:
                    v.tensor_scalar(inv_count[:, :], count[:, :], 1.0, None, ALU.max)
                    v.tensor_scalar(std[:, :], count[:, :], 1.0, 1.0, ALU.add, ALU.max).then_inc(deg_ready, 1)
                    dve.drain()
                    v.reciprocal(inv_count[:, :], inv_count[:, :])
                    dve.wait_ge(deg_root, 1)
                    v.reciprocal(deg_rsqrt[:, :], deg_rsqrt[:, :])
                if p == GCN:
                    dve.drain()
                    v.tensor_copy(w_parts[:, 0, :], w_f[:, :])
                    dve.drain()
                    v.tensor_tensor(w_left, w_f[:, :], w_parts[:, 0, :], ALU.subtract)
                    dve.drain()
                    v.tensor_copy(w_parts[:, 1, :], w_left)
                    dve.drain()
                    v.tensor_tensor(w_parts[:, 2, :], w_left, w_parts[:, 1, :], ALU.subtract)
                parts = 3 if p == SAGE else 1
                oh_slots = OHS_W if p == SAGE else OHS

                def make_onehots(to, g):
                    there = dst_id[:, ds(g * B, B)].rearrange("p (o b) -> p o b", o=1).to_broadcast([P, P, B])
                    if p < SAGE:
                        return v.tensor_tensor(to.rearrange("p (n b) -> p n b", b=B), node_ids[:, :, :], there,
                                               ALU.is_equal)
                    dve.drain()
                    v.tensor_tensor(matches[:, :, :], node_ids[:, :, :], there, ALU.is_equal)
                    dve.drain()
                    for a in range(3):
                        w = w_parts[:, a, :][:, ds(g * B, B)].rearrange("p (o b) -> p o b", o=1)
                        last = v.tensor_tensor(to[:, a * B * P:(a + 1) * B * P].rearrange("p (n b) -> p n b", b=B),
                                               matches[:, :, :], w.to_broadcast([P, P, B]), ALU.mult)
                    return last

                def full_onehots(lo, hi):
                    with dve.If(lo < hi):
                        with dve.Fori(lo, hi) as g:
                            dve.wait_ge(batch_used, g + (FULL * p + CREDIT - oh_slots + 1))
                            if p == SAGE:
                                dve.sem_inc(dve_go, 1)
                            slot = dve.snap((g % oh_slots) * (parts * B * P))
                            make_onehots(onehot[:, ds(slot, parts * B * P)], g).then_inc(onehot_ready, 1)

                def open_of(row, d):
                    return dve.value_load(row[0:1, ds(d, 1)], min_val=0, max_val=FULL)

                def onehots_ahead(d):
                    v.tensor_scalar(node_ids[:, :, :], node_ids[:, :, :], float(P), None, ALU.add)
                    dve.drain()
                    full_onehots(open_of(first_open, d), open_of(ahead_end, d))
                    make_onehots(onehot_edge[:, 0:parts * B * P], open_of(first_open, d + 1)
                                 ).then_inc(edge_ready, 1)

                v.tensor_copy(node_ids[:, :, :], first_ids[:, :, :])
                dve.drain()
                onehots_ahead(0)

                def node_tile(d):
                    full_onehots(open_of(ahead_end, d), open_of(first_open, d + 1))
                    here = NT * p + 1
                    dve.wait_ge(agg_ready, here + d)
                    if p == 0:
                        v.tensor_copy(count[:, ds(d, 1)], ps_count[:, 0:1])
                    if p == SAGE:
                        by_count = inv_count[:, ds(d, 1)]
                        v.tensor_scalar(agg_sum[:, 0:W], ps_agg[:, 2 * W:3 * W], by_count, None, ALU.mult)
                        for part in (1, 0):
                            dve.drain()
                            last = v.scalar_tensor_tensor(out=agg_sum[:, 0:W], in0=ps_agg[:, part * W:(part + 1) * W],
                                                          scalar=by_count, in1=agg_sum[:, 0:W],
                                                          op0=ALU.mult, op1=ALU.add)
                    else:
                        v.tensor_copy(agg_sum[:, 0:W], ps_agg[:, 2 * W:3 * W])
                        for part in (1, 0):
                            dve.drain()
                            last = v.tensor_tensor(agg_sum[:, 0:W], ps_agg[:, part * W:(part + 1) * W],
                                                   agg_sum[:, 0:W], ALU.add)
                    if p in (GIN1, GIN2):
                        dve.drain()
                        last = v.tensor_tensor(agg_sum[:, 0:W], agg_sum[:, 0:W],
                                               tile(x_all if p == GIN1 else gin_h, d), ALU.add)
                    if p == GCN:
                        dve.drain()
                        last = v.scalar_tensor_tensor(out=agg_sum[:, 0:H], in0=tile(x_all, d),
                                                      scalar=deg_rsqrt[:, ds(d, 1)], in1=agg_sum[:, 0:H],
                                                      op0=ALU.mult, op1=ALU.add)
                    last.then_inc(sum_ready, 1)
                    if p == GCN:
                        dve.drain()
                        v.tensor_tensor(tile(x_all, d), tile(x_all, d), beta_all[:, :], ALU.add)
                    if p in (GIN1, GIN2, SAGE):
                        onehots_ahead(d + 1)

                    if p < STEPS:
                        dve.wait_ge(sig_ready, here + d)
                        v.scalar_tensor_tensor(out=cand[:, :], in0=gates[:, 0:H], scalar=1.0,
                                               in1=ps_gates[:, 3 * H:4 * H], op0=ALU.add, op1=ALU.mult)
                        dve.drain()
                        v.scalar_tensor_tensor(out=cand[:, :], in0=cand[:, :], scalar=0.5,
                                               in1=ps_gates[:, 2 * H:3 * H], op0=ALU.mult, op1=ALU.add
                                               ).then_inc(cand_ready, 1)
                        dve.wait_ge(tanh_ready, here + d)
                        v.tensor_tensor(diff[:, :], tile(h_all, d), cand_act[:, :], ALU.subtract)
                        dve.drain()
                        v.scalar_tensor_tensor(out=diff[:, :], in0=gates[:, H:2 * H], scalar=1.0, in1=diff[:, :],
                                               op0=ALU.add, op1=ALU.mult)
                        dve.drain()

                        def new_state(to):
                            return v.scalar_tensor_tensor(out=to, in0=diff[:, :], scalar=0.5, in1=cand_act[:, :],
                                                          op0=ALU.mult, op1=ALU.add)

                        if p < STEPS - 1:
                            new_state(row_new[:, 0:H]).then_inc(row_ready, 1)
                            dve.drain()
                            v.tensor_copy(tile(h_all, d), row_new[:, 0:H])
                            onehots_ahead(d + 1)
                            typed_rows(p, d)
                        else:
                            new_state(y_row[:, :])
                            dve.drain()
                            v.tensor_tensor(y_row[:, :], y_row[:, :], tile(x_all, d), ALU.add)
                            onehots_ahead(d + 1)
                            layernorm(0, d, row_new[:, 0:H]).then_inc(source_ready, 1)
                            dve.drain()
                            v.tensor_copy(tile(x_all, d), row_new[:, 0:H])
                            split(p, d, row_new[:, 0:H].rearrange("p (k w) -> p k w", k=1), 1, H)
                    elif p == GIN1:
                        dve.wait_ge(v_copied, d + 1)
                        v.tensor_copy(tile(gin_h, d), row_new[:, :])
                        split(p, d, row_new[:, :].rearrange("p (k w) -> p k w", k=1), 1, HID)
                    elif p == GIN2:
                        dve.wait_ge(v_copied, NT + 1 + d)
                        v.tensor_tensor(y_row[:, :], v_row[:, :], tile(x_all, d), ALU.add)
                        layernorm(1, d, o_row[:, :])
                        dve.drain()
                        v.tensor_copy(tile(x_all, d), o_row[:, :])
                        v.tensor_scalar(row_new[:, 0:H], o_row[:, :], deg_rsqrt[:, ds(d, 1)], None, ALU.mult
                                        ).then_inc(source_ready, 1)
                        dve.drain()
                        split(p, d, row_new[:, 0:H].rearrange("p (k w) -> p k w", k=1), 1, H)
                    elif p == GCN:
                        dve.wait_ge(o_ready, d + 1)
                        v.scalar_tensor_tensor(out=o_row[:, :], in0=ps_u[:, 0:H], scalar=deg_rsqrt[:, ds(d, 1)],
                                               in1=gcn_b_all[:, :], op0=ALU.mult, op1=ALU.add
                                               ).then_inc(o_biased, 1)
                        onehots_ahead(d + 1)
                        dve.wait_ge(relu_done, d + 1)
                    else:
                        dve.wait_ge(o_ready, NT + 1 + d)
                        v.tensor_tensor(y_row[:, :], ps_v[:, 0:H], tile(x_all, d), ALU.add)
                        layernorm(2, d, out_row[:, :]).then_inc(out_ready, 1)

                if p < GCN:
                    with dve.Fori(0, NT) as d:
                        node_tile(d)
                else:
                    with dve.Fori(0, NT - 1) as d:
                        node_tile(d)
                    node_tile(NT - 1)

                if p == GCN:
                    def over(t, n):
                        return t[:, :].rearrange("p (o f) -> p o f", o=1).to_broadcast([P, n, H])

                    def chunk(c):
                        sq = squares.rearrange("p (d f) -> p d f", f=H)[:, c * CH:(c + 1) * CH, :]
                        return (h_all[:, c * CH:(c + 1) * CH, :], sq, x_all[:, c * CH:(c + 1) * CH, :],
                                ring_stage[:, c % 4])

                    def per_node(t, c):
                        return t[:, c * CH:(c + 1) * CH].rearrange("p (d o) -> p d o", o=1).to_broadcast([P, CH, H])

                    dve.wait_ge(bn_mean, 1)
                    v.tensor_copy(mean_all[:, :], ps_count[:, 0:H])
                    dve.drain()
                    for c in range(NCH):
                        hc, sq, xc, st = chunk(c)
                        last = v.tensor_tensor(hc, hc, over(mean_all, CH), ALU.subtract)
                        if c == NCH - 1:
                            dve.drain()
                            last = v.tensor_scalar(h_all[:, NT - 1, :], h_all[:, NT - 1, :], mask_last[:, :], None,
                                                   ALU.mult)
                        last.then_inc(bn_centred, 1)
                    dve.wait_ge(bn_var, 1)
                    v.tensor_reduce(out=var_all[:, :], in_=ps_u[:, 0:CH * H // 2].rearrange("p (g c) -> p c g", c=H),
                                    axis=AX.X, op=ALU.add).then_inc(bn_var_copied, 1)
                    dve.wait_ge(bn_std, 1)
                    v.reciprocal(var_all[:, :], var_all[:, :])
                    dve.drain()
                    v.tensor_tensor(gamma_all[:, :], gamma_all[:, :], var_all[:, :], ALU.mult
                                    ).then_inc(bn_scale, 1)

                    def centre(c):
                        hc, sq, xc, st = chunk(c)
                        dve.drain()
                        dve.wait_ge(ch_scaled, c + 1)
                        v.tensor_tensor(hc, hc, xc, ALU.add)
                        dve.drain()
                        v.reduce_sum(ln_sum[:, c * CH:(c + 1) * CH], hc, axis=AX.X)
                        dve.drain()
                        v.tensor_scalar(ln_sum[:, c * CH:(c + 1) * CH], ln_sum[:, c * CH:(c + 1) * CH], 1.0 / H, None,
                                        ALU.mult)
                        dve.drain()
                        v.tensor_tensor(hc, hc, per_node(ln_sum, c), ALU.subtract).then_inc(ch_centred, 1)

                    def scale(c):
                        hc, sq, xc, st = chunk(c)
                        dve.wait_ge(ch_squared, c + 1)
                        v.reduce_sum(ln_rstd[:, c * CH:(c + 1) * CH], sq, axis=AX.X).then_inc(ch_var, 1)
                        dve.wait_ge(ch_std, c + 1)
                        v.reciprocal(ln_rstd[:, c * CH:(c + 1) * CH], std[:, c * CH:(c + 1) * CH])
                        dve.drain()
                        v.tensor_tensor(xc, hc, per_node(ln_rstd, c), ALU.mult).then_inc(ch_done, 1)

                    for c in range(NCH + 1):
                        if c < NCH:
                            centre(c)
                        if c >= 1:
                            scale(c - 1)


_INS = ['x', 'src', 'dst', 'edge_type_4', 'edge_weight', 'L0_gnn_W', 'L0_gnn_b', 'L0_gnn_w_ih', 'L0_gnn_w_hh',
        'L0_gnn_b_ih', 'L0_gnn_b_hh', 'L1_gnn_W1a', 'L1_gnn_b1a', 'L1_gnn_W1b', 'L1_gnn_b1b', 'L1_gnn_W2a',
        'L1_gnn_b2a', 'L1_gnn_W2b', 'L1_gnn_b2b', 'L2_gnn_W', 'L2_gnn_b', 'L2_gnn_gamma', 'L2_gnn_beta',
        'L3_gnn_W_self', 'L3_gnn_b_self', 'L3_gnn_W_neigh', 'L3_gnn_b_neigh']


def kernel(**inputs):
    import numpy as _np
    import concourse.bacc as _bacc
    from concourse import mybir as _mybir
    from concourse.bass_utils import run_bass_kernel_spmd as _run

    nc = _bacc.Bacc("TRN2", target_bir_lowering=False, num_devices=1)
    arrays, args = {}, []
    for name in _INS:
        a = _np.ascontiguousarray(inputs[name])
        arrays[f"in_{name}"] = a
        args.append(nc.dram_tensor(f"in_{name}", a.shape, _mybir.dt.from_np(a.dtype), kind="ExternalInput").ap())
    out = nc.dram_tensor("out_0", (N, H), _mybir.dt.float32, kind="ExternalOutput").ap()
    build(nc, *args, out)
    r = _run(nc, [arrays], core_ids=[0])
    return r.results[0]["out_0"]
```
